# Optimizing a Trainium2 kernel written in Bass

```python
import numpy as np
import jax
import jax.numpy as jnp

def _softmax(x, axis=-1):
    return jax.nn.softmax(x, axis=axis)

def _gelu(x):
    return jax.nn.gelu(x, approximate=True)

def _silu(x):
    return jax.nn.silu(x)

def _sigmoid(x):
    return jax.nn.sigmoid(x)

def _layernorm(x, axis=-1, eps=1e-05):
    m = jnp.mean(x, axis=axis, keepdims=True)
    v = jnp.var(x, axis=axis, keepdims=True)
    return (x - m) / jnp.sqrt(v + eps)

def _scatter_add(tgt, idx, src, axis=0):
    return tgt.at[idx].add(src)

def _segment_sum(src, seg, n):
    return jax.ops.segment_sum(src, seg, n)
kernel_name = 'mk_lm_tower_d1_tok_ids512_r4_312ec1'

def setup_inputs(seed: int=0):
    np.random.seed(seed)
    _w = jnp.asarray

    def _rec_inputs():
        import jax
        import jax.numpy as jnp
        _rk = jax.random.key(seed)
        x = jax.random.randint(jax.random.fold_in(_rk, 1), (128, 128), 0, 10000, jnp.int32)
        return x
    x = _rec_inputs()

    def _L0_tok_setup():
        import jax, jax.numpy as jnp
        import numpy as np
        B, S, H = (64, 512, 128)
        VOCAB = 10000

        def _syntax_info(token_ids):
            t = token_ids
            opens = (t == 40) | (t == 123) | (t == 91)
            closes = (t == 41) | (t == 125) | (t == 93)
            delta = opens.astype(jnp.int32) - closes.astype(jnp.int32)
            s = jnp.cumsum(delta, axis=1)
            run_min = jax.lax.cummin(s, axis=1)
            nesting = jnp.clip(s - jnp.minimum(run_min, 0), 0, 15)
            segments = jnp.cumsum((t > 39990).astype(jnp.int32), axis=1) % 8
            return (nesting, segments)
        key = jax.random.key(seed)
        k1, k2, k3, k4, k5 = jax.random.split(key, 5)
        token_ids = jax.random.randint(k1, (B, S), 0, VOCAB, dtype=jnp.int64) if jax.config.jax_enable_x64 else jax.random.randint(k1, (B, S), 0, VOCAB, dtype=jnp.int32)
        std = 0.02
        pos_table = jax.random.normal(k2, (S, H), dtype=jnp.float32) * std
        nest_table = jax.random.normal(k3, (16, H), dtype=jnp.float32) * std
        seg_table = jax.random.normal(k4, (8, H), dtype=jnp.float32) * std
        W = jax.random.normal(k5, (3 * H, H), dtype=jnp.float32) * (1.0 / np.sqrt(3 * H))
        return {'token_ids': token_ids, 'pos_table': pos_table, 'nest_table': nest_table, 'seg_table': seg_table, 'W': W}
    _L0_tok_all = _L0_tok_setup()
    _L0_tok_in = {k: v for k, v in _L0_tok_all.items() if k in ('pos_table', 'nest_table', 'seg_table', 'W')}
    del _L0_tok_all

    def _L0_attn_setup():
        import jax, jax.numpy as jnp
        import numpy as np
        BLOCK = 128
        C = 32
        NEG_INF = -10000000000.0

        def build_sparse_mask(n):
            r = np.arange(n)
            q = r[:, None]
            k = r[None, :]
            lower = k <= q
            m1 = np.floor_divide(q, BLOCK) == np.floor_divide(k, BLOCK)
            rem = np.remainder(k, BLOCK)
            m2 = np.logical_or(rem == 0, rem >= BLOCK - C)
            mask = np.logical_or(np.logical_and(lower, m1), np.logical_and(lower, m2))
            return mask[None, None]
        key = jax.random.key(seed)
        ks = jax.random.split(key, 5)
        B, S, D, H, HD = (2, 1024, 128, 8, 64)
        scale = 0.02
        return {'inputs_q': jax.random.normal(ks[0], (B, S, D), jnp.float32), 'wq': jax.random.normal(ks[1], (D, H, HD), jnp.float32) * scale, 'bq': jnp.zeros((H, HD), jnp.float32), 'wk': jax.random.normal(ks[2], (D, H, HD), jnp.float32) * scale, 'bk': jnp.zeros((H, HD), jnp.float32), 'wv': jax.random.normal(ks[3], (D, H, HD), jnp.float32) * scale, 'bv': jnp.zeros((H, HD), jnp.float32), 'wo': jax.random.normal(ks[4], (H, HD, D), jnp.float32) * scale, 'bo': jnp.zeros((D,), jnp.float32)}
    _L0_attn_all = _L0_attn_setup()
    _L0_attn_in = {k: v for k, v in _L0_attn_all.items() if k in ('wq', 'bq', 'wk', 'bk', 'wv', 'bv', 'wo', 'bo')}
    del _L0_attn_all

    def _L0_ffn_setup():
        import jax, jax.numpy as jnp
        import numpy as np
        TOP_K = 2
        key = jax.random.key(seed)
        ks = jax.random.split(key, 4)
        b, t, d, e, h = (2, 512, 128, 8, 256)
        scale = 0.02
        return {'x': jax.random.normal(ks[0], (b, t, d), dtype=jnp.float32), 'router_w': jax.random.normal(ks[1], (e, d), dtype=jnp.float32) * scale, 'router_b': jnp.zeros((e,), dtype=jnp.float32), 'fc1_w': jax.random.normal(ks[2], (e, 2 * h, d), dtype=jnp.float32) * scale, 'fc1_b': jnp.zeros((e, 2 * h), dtype=jnp.float32), 'fc2_w': jax.random.normal(ks[3], (e, d, h), dtype=jnp.float32) * scale, 'fc2_b': jnp.zeros((e, d), dtype=jnp.float32)}
    _L0_ffn_all = _L0_ffn_setup()
    _L0_ffn_in = {k: v for k, v in _L0_ffn_all.items() if k in ('router_w', 'router_b', 'fc1_w', 'fc1_b', 'fc2_w', 'fc2_b')}
    del _L0_ffn_all
    return {'x': x, 'L0_tok_pos_table': _L0_tok_in['pos_table'], 'L0_tok_nest_table': _L0_tok_in['nest_table'], 'L0_tok_seg_table': _L0_tok_in['seg_table'], 'L0_tok_W': _L0_tok_in['W'], 'L0_attn_wq': _L0_attn_in['wq'], 'L0_attn_bq': _L0_attn_in['bq'], 'L0_attn_wk': _L0_attn_in['wk'], 'L0_attn_bk': _L0_attn_in['bk'], 'L0_attn_wv': _L0_attn_in['wv'], 'L0_attn_bv': _L0_attn_in['bv'], 'L0_attn_wo': _L0_attn_in['wo'], 'L0_attn_bo': _L0_attn_in['bo'], 'L0_ffn_router_w': _L0_ffn_in['router_w'], 'L0_ffn_router_b': _L0_ffn_in['router_b'], 'L0_ffn_fc1_w': _L0_ffn_in['fc1_w'], 'L0_ffn_fc1_b': _L0_ffn_in['fc1_b'], 'L0_ffn_fc2_w': _L0_ffn_in['fc2_w'], 'L0_ffn_fc2_b': _L0_ffn_in['fc2_b']}

def reference(x, L0_tok_pos_table, L0_tok_nest_table, L0_tok_seg_table, L0_tok_W, L0_attn_wq, L0_attn_bq, L0_attn_wk, L0_attn_bk, L0_attn_wv, L0_attn_bv, L0_attn_wo, L0_attn_bo, L0_ffn_router_w, L0_ffn_router_b, L0_ffn_fc1_w, L0_ffn_fc1_b, L0_ffn_fc2_w, L0_ffn_fc2_b):
    import jax
    import jax.numpy as jnp

    def _L0_tok_ref(token_ids, pos_table, nest_table, seg_table, W):
        import jax, jax.numpy as jnp
        import numpy as np
        B, S, H = (64, 512, 128)
        VOCAB = 10000

        def _syntax_info(token_ids):
            t = token_ids
            opens = (t == 40) | (t == 123) | (t == 91)
            closes = (t == 41) | (t == 125) | (t == 93)
            delta = opens.astype(jnp.int32) - closes.astype(jnp.int32)
            s = jnp.cumsum(delta, axis=1)
            run_min = jax.lax.cummin(s, axis=1)
            nesting = jnp.clip(s - jnp.minimum(run_min, 0), 0, 15)
            segments = jnp.cumsum((t > 39990).astype(jnp.int32), axis=1) % 8
            return (nesting, segments)
        b, s = token_ids.shape
        positions = jnp.arange(s)
        pos_emb = jnp.broadcast_to(pos_table[positions][None], (b, s, pos_table.shape[-1]))
        nesting, segments = _syntax_info(token_ids)
        nest_emb = nest_table[nesting]
        seg_emb = seg_table[segments]
        combined = jnp.concatenate([pos_emb, nest_emb, seg_emb], axis=-1)
        return jnp.einsum('bsk,kh->bsh', combined, W)

    def _L0_attn_ref(inputs_q, wq, bq, wk, bk, wv, bv, wo, bo):
        import jax, jax.numpy as jnp
        import numpy as np
        BLOCK = 128
        C = 32
        NEG_INF = -10000000000.0

        def build_sparse_mask(n):
            r = np.arange(n)
            q = r[:, None]
            k = r[None, :]
            lower = k <= q
            m1 = np.floor_divide(q, BLOCK) == np.floor_divide(k, BLOCK)
            rem = np.remainder(k, BLOCK)
            m2 = np.logical_or(rem == 0, rem >= BLOCK - C)
            mask = np.logical_or(np.logical_and(lower, m1), np.logical_and(lower, m2))
            return mask[None, None]
        B, S, D = inputs_q.shape
        q = jnp.einsum('bsd,dhk->bshk', inputs_q, wq) + bq
        k = jnp.einsum('bsd,dhk->bshk', inputs_q, wk) + bk
        v = jnp.einsum('bsd,dhk->bshk', inputs_q, wv) + bv
        head_dim = q.shape[-1]
        q = q / jnp.sqrt(jnp.asarray(head_dim, q.dtype))
        logits = jnp.einsum('bqhd,bkhd->bhqk', q, k)
        mask = jnp.asarray(build_sparse_mask(S))
        logits = jnp.where(mask, logits, jnp.asarray(NEG_INF, logits.dtype))
        weights = jax.nn.softmax(logits, axis=-1)
        x = jnp.einsum('bhqk,bkhd->bqhd', weights, v)
        out = jnp.einsum('bqhd,hdf->bqf', x, wo) + bo
        return out

    def _L0_ffn_ref(x, router_w, router_b, fc1_w, fc1_b, fc2_w, fc2_b):
        import jax, jax.numpy as jnp
        import numpy as np
        TOP_K = 2
        n_experts = router_w.shape[0]
        temp = 1.0
        logits = (jnp.einsum('btd,ed->bte', x, router_w) + router_b) / temp
        topk_val, topk_idx = jax.lax.top_k(logits, TOP_K)
        weights = jax.nn.softmax(topk_val, axis=-1)
        onehot = jax.nn.one_hot(topk_idx, n_experts, dtype=x.dtype)
        cw = jnp.einsum('btk,btke->bte', weights, onehot)
        h = jnp.einsum('btd,efd->btef', x, fc1_w) + fc1_b
        h1, h2 = jnp.split(h, 2, axis=-1)
        a = jax.nn.silu(h1) * h2
        y = jnp.einsum('bteh,edh->bted', a, fc2_w) + fc2_b
        out = jnp.einsum('bted,bte->btd', y, cw)
        return out
    h = _L0_tok_ref(x, L0_tok_pos_table, L0_tok_nest_table, L0_tok_seg_table, L0_tok_W)
    h = h + _L0_attn_ref(_layernorm(h, axis=-1), L0_attn_wq, L0_attn_bq, L0_attn_wk, L0_attn_bk, L0_attn_wv, L0_attn_bv, L0_attn_wo, L0_attn_bo)
    h = h + _L0_ffn_ref(_layernorm(h, axis=-1), L0_ffn_router_w, L0_ffn_router_b, L0_ffn_fc1_w, L0_ffn_fc1_b, L0_ffn_fc2_w, L0_ffn_fc2_b)
    return h

_drawn_inputs = setup_inputs


def setup_inputs(seed=0):
    import zlib

    import numpy as np

    out = dict(_drawn_inputs(seed))
    spreads = {'L0_attn_bq': (0.0, 0.8),
     'L0_attn_bk': (0.0, 0.8),
     'L0_attn_bv': (0.0, 0.1),
     'L0_attn_bo': (0.0, 0.1),
     'L0_ffn_router_b': (0.0, 0.1),
     'L0_ffn_fc1_b': (0.0, 0.334),
     'L0_ffn_fc2_b': (0.0, 0.1)}
    factors = {'L0_attn_wq': 7.574}
    for name, (base, spread) in spreads.items():
        noise = np.random.default_rng([zlib.crc32(name.encode()), seed]).standard_normal(out[name].shape)
        drawn = base * np.exp(spread * noise) if base else spread * noise
        out[name] = jnp.asarray(drawn.astype(out[name].dtype))
    for name, factor in factors.items():
        out[name] = (out[name] * factor).astype(out[name].dtype)
    return out
```

```python
import numpy as np
import concourse.bass as bass
from concourse import mybir
from concourse.alu_op_type import AluOpType as ALU
from contextlib import ExitStack

S = 128
D = 128
HEADS, HD = 8, 64
PAIRS = HEADS // 2
NEST, SEG = 16, 8
PARTS = 3
CODES = PARTS * (NEST + SEG)
EXPERTS, HID = 8, 256
FC1 = 2 * HID
GB = 4
OB = 2 * GB
NEG_INF = -10000000000.0
HUGE = 3.0e38
EPS = 1e-5
TABLE_STEPS = 13
SW_LEAD = 16
LEAD = 64


def octet_steps(previous):
    steps = []

    def late(*step):
        if step[1] >= 0 or previous:
            steps.append(step)

    for k in range(OB):
        half, n = k // GB, k % GB
        g = half - 1
        steps.append(("scores", k))
        late("project", k - 2)
        steps.append(("query", half + 1, n))
        steps.append(("max", k))
        late("probsT", k - 1)
        steps.append(("value", half + 1, n))
        late("mix", k - 1)
        steps.append(("exp", k, 0))
        steps.append(("key", half + 1, n))
        if n == 0:
            late("route_ranks", g - 1)
        elif n == 1:
            late("route_norm", g)
            steps.append(("onehot", half + 2))
        elif n == 2:
            late("route_normT", g)
        elif n == 3:
            late("route_logits", g)
        late("mixT", k - 1)
        steps.append(("exp", k, 1))
        if n == 0:
            late("route_rows", g - 1)
            late("scatter", g - 1, 0)
        elif n == 1:
            steps.append(("embed", half + 2))
            steps.append(("residual", half + 1))
            late("route_weight", g - 1)
            late("route_scale", g)
        elif n == 2:
            steps.append(("norm", half + 2))
            late("scatter", g - 1, 1)
        elif n == 3:
            steps.append(("normT", half + 2))
            late("route_choose", g)
    return steps


def last_steps():
    return [(st[0], st[1] + (OB if st[0] in ("project", "probsT", "mix", "mixT") else 2), *st[2:])
            for st in octet_steps(True) if st[1] < 0]


def first_steps():
    return ([(w, g) for g in range(2) for w in ("onehot", "embed", "norm", "normT")] + [("residual", 0)] +
            [(w, 0, n) for n in range(PAIRS) for w in ("query", "value", "key")])


def build(nc, a, out, hmid, codes_dram, xs, ys, spare, nseq):
    F32, F32R, BF16, I32 = mybir.dt.float32, mybir.dt.float32r, mybir.dt.bfloat16, mybir.dt.int32
    ACT = mybir.ActivationFunctionType
    AX = mybir.AxisListType.X
    groups = nseq // GB
    octets = nseq // OB
    chunks = 4 if nseq == 128 else 2
    per_chunk = octets // chunks
    U32 = mybir.dt.uint32
    R = per_chunk * OB * S + S
    TILES = 2 * per_chunk * OB + EXPERTS
    ctx = ExitStack()
    with ctx:
        def sb(name, shape, dt=F32):
            return ctx.enter_context(nc.sbuf_tensor(name, shape, dt))

        def sem(name):
            return ctx.enter_context(nc.semaphore(name))

        led = []

        def led_sem(name):
            s = sem(name)
            led.append(s)
            return s

        ident = sb("ident", [128, 128])
        causal = sb("causal", [128, 128])
        part_code = sb("part_code", [CODES, 1])
        part_mask = sb("part_mask", [CODES, PARTS])
        small = sb("small", [CODES, 4])
        posT = sb("posT", [128, S]); nestT = sb("nestT", [128, CODES]); segT = sb("segT", [128, CODES])
        w_emb = sb("w_emb", [128, 3, D])
        pos_emb = sb("pos_emb", [S, D])
        code_table = sb("code_table", [CODES, D], BF16)
        w_hi = sb("w_hi", [128, 3, HEADS * HD], F32R)
        w_lo = sb("w_lo", [128, 3, HEADS * HD], F32R)
        bias_qk = sb("bias_qk", [128, 2, PAIRS])
        bias_q8 = sb("bias_q8", [128, PAIRS])
        bias_v = sb("bias_v", [128, HEADS * HD])
        bias_o = sb("bias_o", [128, D])
        w_o = sb("w_o", [128, PAIRS, D])

        code_rows = [sb(f"code_rows{i}", [CODES, GB * S], BF16) for i in range(2)]
        onehot = sb("onehot", [CODES, GB * S], BF16)
        h = [sb(f"h{i}", [S, GB, D]) for i in range(2)]
        stats = sb("stats", [S, GB, 6]); moments = sb("moments", [S, GB, 2])
        var_eps = sb("var_eps", [S, GB]); rstd = sb("rstd", [S, GB]); minus_half = sb("minus_half", [S, GB])
        normed = sb("normed", [S, GB, D])
        xT_hi = [sb(f"xT_hi{i}", [D, GB * S], F32R) for i in range(2)]
        xT_lo = [sb(f"xT_lo{i}", [D, GB * S], F32R) for i in range(2)]
        qT = [sb(f"qT{i}", [128, PAIRS, GB * S]) for i in range(2)]
        kT = [sb(f"kT{i}", [128, PAIRS, GB * S]) for i in range(2)]
        v = [sb(f"v{i}", [S, GB, HEADS * HD]) for i in range(2)]

        taken = [0, 0]

        def scratch(room, parts, cols, dt=F32):
            at = taken[room]
            n = cols // 2 if dt == BF16 else cols
            taken[room] += n
            t = v[room][0:parts].rearrange("p a b -> p (a b)")[:, at:at + n]
            return t if dt == F32 else t.bitcast(dt)

        x_raw = scratch(0, nseq, S, I32)
        scan = [scratch(0, nseq, S) for _ in range(4)]
        seg_int = scratch(0, nseq, S, I32)
        codes_sb = scratch(0, nseq, 2 * S, BF16).rearrange("p (a s) -> p a s", a=2)
        t_full, t_rest, t_rest2, t_acc = [scratch(0, CODES, D) for _ in range(4)]
        t_hi, t_mid, t_lo = [scratch(0, CODES, D, BF16) for _ in range(3)]
        b12, b_rest = [scratch(1, PARTS * EXPERTS, FC1 + D) for _ in range(2)]
        b_hi, b_mid = [scratch(1, PARTS * EXPERTS, FC1 + D, BF16) for _ in range(2)]
        b_parts = scratch(0, PARTS * EXPERTS, FC1 + D, BF16)
        w_raw = qT[0][:, 0:3]

        masked = [sb(f"masked{i}", [S, HEADS, S]) for i in range(2)]
        neg_max = [sb(f"neg_max{i}", [S, HEADS]) for i in range(2)]
        probs = [sb(f"probs{i}", [S, HEADS, S]) for i in range(2)]
        sums = [sb(f"sums{i}", [S, HEADS]) for i in range(2)]
        inv_sums = sb("inv_sums", [S, HEADS])
        probsT = sb("probsT", [S, HEADS, S])
        mixed = sb("mixed", [S, HEADS * HD])
        mixedT = sb("mixedT", [128, PAIRS, S])
        h2 = [sb(f"h2_{i}", [S, GB, D]) for i in range(2)]
        residual = [sb(f"residual{i}", [S, GB, D]) for i in range(2)]

        earlier = sb("earlier", [128, 128], BF16)
        ones = sb("ones", [128, 128], BF16)
        expert_no = sb("expert_no", [S, EXPERTS])
        region = sb("region", [S, EXPERTS])
        w_router = sb("w_router", [D, EXPERTS]); bias_r = sb("bias_r", [S, EXPERTS])
        moments2 = sb("moments2", [S, GB, 2]); stats2 = sb("stats2", [S, GB, 6])
        var_eps2 = sb("var_eps2", [S, GB]); rstd2 = sb("rstd2", [S, GB])
        normed2 = [sb(f"normed2_{i}", [S, GB, D]) for i in range(2)]
        x2T = sb("x2T", [D, GB * S])
        logits = sb("logits", [S, GB, EXPERTS]); top = sb("top", [S, GB, EXPERTS]); top_at = sb("top_at", [S, GB, EXPERTS], U32)
        top_no = sb("top_no", [S, GB, 2]); chosen = sb("chosen", [S, 2, GB, EXPERTS]); picked = sb("picked", [S, GB, EXPERTS], BF16)
        gap = sb("gap", [S, GB]); gap_exp = sb("gap_exp", [S, GB]); gap_one = sb("gap_one", [S, GB])
        ranks = sb("ranks", [S, 2, GB, EXPERTS]); filled = sb("filled", [S, GB + 1, EXPERTS])
        rows_f = sb("rows_f", [S, GB, EXPERTS]); rows_2 = sb("rows_2", [S, 2, GB, EXPERTS]); row_f = sb("row_f", [S, 2, GB])
        row = [sb(f"row{i}", [S, 2, GB], I32) for i in range(2)]
        weight = sb("weight", [S, 2, GB])
        rows_all = sb("rows_all", [S, 2, per_chunk * OB], I32)
        weights_all = sb("weights_all", [S, 2, per_chunk * OB])
        ends = sb("ends", [1, EXPERTS], I32)
        tile_no = sb("tile_no", [1, TILES]); tiles_f = sb("tiles_f", [1, EXPERTS]); tiles_i = sb("tiles_i", [1, EXPERTS], I32)
        tiles_end = sb("tiles_end", [1, EXPERTS]); passed = masked[0][0:1].rearrange("p a b -> p (a b)")[:, 0:TILES * EXPERTS].rearrange("p (t e) -> p t e", e=EXPERTS)
        tab = sb("tab", [1, 4, TILES]); tile_row = sb("tile_row", [1, TILES], I32); tile_expert = sb("tile_expert", [1, TILES], I32)
        zeros = sb("zeros", [S, D])

        w1_hi = sb("w1_hi", [D, EXPERTS * FC1], F32R); w1_lo = sb("w1_lo", [D, EXPERTS * FC1], F32R)
        w1_raw = [kT[1], qT[1]]
        w2 = sb("w2", [128, EXPERTS * 2 * D])
        b_mask = sb("b_mask", [PARTS * EXPERTS, PARTS])
        b1_parts = sb("b1_parts", [PARTS, EXPERTS * FC1], BF16); b2_parts = sb("b2_parts", [PARTS, EXPERTS * D], BF16)
        xt = [sb(f"xt{i}", [S, D]) for i in range(4)]
        x3_hi = [sb(f"x3_hi{i}", [D, S], F32R) for i in range(2)]; x3_lo = [sb(f"x3_lo{i}", [D, S], F32R) for i in range(2)]
        gate = [sb(f"gate{i}", [S, HID]) for i in range(2)]; act_out = [sb(f"act_out{i}", [S, HID]) for i in range(2)]
        actT = [sb(f"actT{i}", [128, 2, S]) for i in range(2)]
        y = [sb(f"y{i}", [S, D]) for i in range(4)]

        rows_now = sb("rows_now", [S, 2, OB], I32); weights_now = sb("weights_now", [S, 2, OB])
        y_rows = sb("y_rows", [S, 2, OB, D]); h_back = sb("h_back", [S, OB, D])

        ps = ctx.enter_context(nc.psum_tensor("ps", [128, 8, 512], F32))
        SCORES, PROBST, MIX, MIXT, QK, ROT = 0, 2, 4, 5, 6, 7

        s_const = sem("s_const"); s_x = sem("s_x"); s_w = sem("s_w"); s_wqkv = sem("s_wqkv"); s_codes = sem("s_codes")
        s_codes_out = sem("s_codes_out"); s_pool = sem("s_pool"); s_dve = sem("s_dve"); s_table_ps = sem("s_table_ps")
        s_table = sem("s_table"); s_whi = sem("s_whi"); s_wlo = sem("s_wlo"); s_out = sem("s_out")
        codes_in = [led_sem("codes_in0"), led_sem("codes_in1")]
        onehot_ready = led_sem("onehot_ready"); embed_full = led_sem("embed_full"); embedded = led_sem("embedded")
        moments_ready = led_sem("moments_ready"); normed_ready = led_sem("normed_ready"); normT_full = led_sem("normT_full")
        xhi_ready = led_sem("xhi_ready"); xlo_ready = led_sem("xlo_ready")
        qk_full = led_sem("qk_full"); qk_ready = led_sem("qk_ready"); v_full = led_sem("v_full"); v_ready = led_sem("v_ready")
        scores_full = led_sem("scores_full"); masked_ready = led_sem("masked_ready"); max_ready = led_sem("max_ready")
        probs_ready = led_sem("probs_ready"); pTa_full = led_sem("pTa_full"); pTb_full = led_sem("pTb_full")
        pTa_ready = led_sem("pTa_ready"); pTb_ready = led_sem("pTb_ready"); mix_full = led_sem("mix_full")
        mixed_ready = led_sem("mixed_ready"); mixT_full = led_sem("mixT_full"); mixT_ready = led_sem("mixT_ready")
        project_full = led_sem("project_full"); h2_ready = led_sem("h2_ready")
        h2_stored = [led_sem("h2_stored0"), led_sem("h2_stored1")]
        var_ready = led_sem("var_ready"); var2_ready = led_sem("var2_ready"); rstd_ready = led_sem("rstd_ready"); rstd2_ready = led_sem("rstd2_ready")
        bn_done = led_sem("bn_done"); inv_ready = led_sem("inv_ready"); h2_part = led_sem("h2_part")
        p_own = sem("p_own")
        residual_ready = led_sem("residual_ready")
        bn2_done = led_sem("bn2_done"); moments2_ready = led_sem("moments2_ready"); normed2_ready = led_sem("normed2_ready")
        x2T_full = led_sem("x2T_full"); x2T_ready = led_sem("x2T_ready"); logits_full = led_sem("logits_full")
        logits_ready = led_sem("logits_ready"); top_ready = led_sem("top_ready"); top_at_ready = led_sem("top_at_ready")
        top_no_ready = led_sem("top_no_ready"); gap_ready = led_sem("gap_ready"); chosen_ready = led_sem("chosen_ready")
        picked_ready = led_sem("picked_ready"); gap_exp_ready = led_sem("gap_exp_ready")
        gap_one_ready = led_sem("gap_one_ready"); weight0_ready = led_sem("weight0_ready"); weight1_ready = led_sem("weight1_ready")
        weights_kept = led_sem("weights_kept"); ranks_full = led_sem("ranks_full"); ranks_ready = led_sem("ranks_ready")
        filled_step = led_sem("filled_step"); rows_a = led_sem("rows_a"); rows_b = led_sem("rows_b"); rows_c = led_sem("rows_c")
        row_ready = led_sem("row_ready"); rows_kept = led_sem("rows_kept"); filled_next = led_sem("filled_next")
        scattered = [sem("scattered0"), sem("scattered1")]
        filled_start = led_sem("filled_start"); ends_ready = led_sem("ends_ready"); padded = led_sem("padded")
        table_own = led_sem("table_own"); table_ready = led_sem("table_ready")
        xt_in = [led_sem(f"xt_in{i}") for i in range(4)]
        x3T_full = led_sem("x3T_full"); x3hi_ready = led_sem("x3hi_ready"); x3lo_ready = led_sem("x3lo_ready")
        fc1_full = led_sem("fc1_full"); gate_ready = led_sem("gate_ready"); act_ready = led_sem("act_ready")
        actT_full = led_sem("actT_full"); actT_ready = led_sem("actT_ready"); fc2_full = led_sem("fc2_full")
        y_ready = led_sem("y_ready"); y_stored = [led_sem(f"y_stored{i}") for i in range(4)]
        rows_now_ready = led_sem("rows_now_ready"); weights_now_ready = led_sem("weights_now_ready")
        y_in = sem("y_in"); h_in = led_sem("h_in"); half_total = led_sem("half_total"); total_ready = led_sem("total_ready")
        out_stored = led_sem("out_stored")
        s_w1 = sem("s_w1"); s_w1hi = sem("s_w1hi"); s_w1lo = sem("s_w1lo"); s_bias = sem("s_bias"); s_bparts = sem("s_bparts")
        s_bmoved = sem("s_bmoved"); s_zero = sem("s_zero"); s_yzero = sem("s_yzero"); wait_carried = sem("wait_carried"); s_trash = sem("s_trash"); s_pool2 = sem("s_pool2")

        block = ctx.enter_context(nc.Block())
        hview = hmid.rearrange("(g j) s d -> g s j d", j=GB)

        def carry_wait(eng):
            eng.sem_inc(wait_carried, 1)

        XB, HB, AB, YB = 0, 2, 4, 6

        def each_tile(eng, c, tile, kinds, lags):
            def at(q, m):
                tile(c, q, m, [x for x, lag in zip(kinds, lags) if 0 <= 4 * q + m - lag < TILES])
            for m in range(4):
                at(0, m)
            with eng.Fori(1, TILES // 4) as q:
                for m in range(4):
                    tile(c, q, m, kinds)
            for m in range(max(lags)):
                at(TILES // 4, m)

        @block.sync
        def _(sp):
            for s in led:
                sp.sem_inc(s, LEAD)
            sp.dma_start(x_raw[:], a["x"]).then_inc(s_x, 16)
            sp.dma_start(posT[:], a["posT"]).then_inc(s_w, 16)
            sp.dma_start(w_emb[:], a["w_emb"].rearrange("(c p) n -> p c n", c=3)).then_inc(s_w, 16)
            sp.dma_start(nestT[:], a["nestT"]).then_inc(s_w, 16)
            sp.dma_start(segT[:], a["segT"]).then_inc(s_w, 16)
            for n, w in enumerate(("wq", "wk", "wv")):
                sp.dma_start(w_raw[:, n], a[w]).then_inc(s_wqkv, 16)
            sp.dma_start(bias_qk[:, 0], a["bq"]).then_inc(s_wqkv, 16)
            sp.dma_start(bias_qk[:, 1], a["bk"]).then_inc(s_wqkv, 16)
            sp.dma_start(bias_v[:], a["bv"].broadcast_to([128, HEADS * HD])).then_inc(s_wqkv, 16)
            sp.dma_start(bias_o[:], a["bo"].broadcast_to([128, D])).then_inc(s_wqkv, 16)
            sp.dma_start(w_o[:], a["wo"].rearrange("(c p) n -> p c n", c=PAIRS)).then_inc(s_wqkv, 16)
            sp.dma_start(w1_raw[0][:].rearrange("p a b -> p (a b)"), a["w1"][:, 0:EXPERTS * FC1 // 2]).then_inc(s_w1, 16)
            sp.dma_start(w1_raw[1][:].rearrange("p a b -> p (a b)"), a["w1"][:, EXPERTS * FC1 // 2:]).then_inc(s_w1, 16)
            sp.dma_start(w2[:], a["w2"]).then_inc(s_w1, 16)
            sp.dma_start(w_router[:], a["wr"]).then_inc(s_w1, 16)
            sp.dma_start(bias_r[:], a["br"].broadcast_to([S, EXPERTS])).then_inc(s_w1, 16)
            for n in range(PARTS):
                sp.dma_start(b12[n * EXPERTS:(n + 1) * EXPERTS, 0:FC1], a["b1"]).then_inc(s_bias, 16)
                sp.dma_start(b12[n * EXPERTS:(n + 1) * EXPERTS, FC1:], a["b2"]).then_inc(s_bias, 16)
            sp.wait_ge(s_zero, 1)
            for n in range(EXPERTS):
                sp.dma_start(xs[EXPERTS * R + n * S:EXPERTS * R + (n + 1) * S], zeros[:]).then_inc(s_trash, 16)
            sp.wait_ge(s_trash, 16 * EXPERTS)
            sp.wait_ge(s_bparts, 1)
            for n in range(PARTS):
                sp.dma_start(b1_parts[n:n + 1].rearrange("p (e n) -> p e n", e=EXPERTS), b_parts[n * EXPERTS:(n + 1) * EXPERTS, 0:FC1]).then_inc(s_bmoved, 16)
                sp.dma_start(b2_parts[n:n + 1].rearrange("p (e n) -> p e n", e=EXPERTS), b_parts[n * EXPERTS:(n + 1) * EXPERTS, FC1:]).then_inc(s_bmoved, 16)
            sp.wait_ge(s_codes, 2)
            cd = codes_dram.rearrange("k (b s) -> b k s", s=S)
            sp.dma_start(cd[0:nseq], codes_sb[:]).then_inc(s_codes_out, 16)
            sp.dma_start(cd[nseq:nseq + OB], codes_sb[0:OB]).then_inc(s_codes_out, 16)
            sp.wait_ge(s_codes_out, 32)

            def load_codes(G, par):
                sp.wait_ge(onehot_ready, LEAD + G - 1)
                sp.dma_start(code_rows[par][0:PARTS * NEST], codes_dram[0:1, bass.ds(G * GB * S, GB * S)].broadcast_to([PARTS * NEST, GB * S])).then_inc(codes_in[par], 16)
                sp.dma_start(code_rows[par][PARTS * NEST:CODES], codes_dram[1:2, bass.ds(G * GB * S, GB * S)].broadcast_to([PARTS * SEG, GB * S])).then_inc(codes_in[par], 16)

            def octet(o, steps):
                for st in steps:
                    if st == ("scores", 0):
                        load_codes(2 * o + 2, 0)
                    if st == ("scores", 4):
                        load_codes(2 * o + 3, 1)
                    if st[0] == "route_norm":
                        G = 2 * o + st[1]
                        sp.wait_ge(h2_ready, LEAD + GB * (G + 1))
                        sp.dma_start(hview[G], h2[st[1] % 2][:]).then_inc(h2_stored[st[1] % 2], 16)

            def pad(c):
                sp.wait_ge(ends_ready, LEAD + c + 1)
                carry_wait(sp)
                for e in range(EXPERTS):
                    end = sp.value_load(ends[0:1, e:e + 1], min_val=0, max_val=EXPERTS * R - S)
                    sp.dma_start(xs[bass.ds(end, S)], zeros[:]).then_inc(padded, 16)
                sp.wait_ge(padded, LEAD + 16 * EXPERTS * (c + 1))
                for par in range(2):
                    sp.wait_ge(scattered[par], SW_LEAD + 16 * 2 * GB * per_chunk * (c + 1))
                sp.wait_ge(table_ready, LEAD + 2 * (c + 1))

            def tile(c, q, m, load=True, store=True):
                i = 4 * q
                n = c * TILES + i + m
                if load:
                    sp.wait_ge(x3T_full, LEAD + n - 3)
                    carry_wait(sp)
                    first = sp.value_load(tile_row[0:1, bass.ds(i + m, 1)], min_val=0, max_val=EXPERTS * R + EXPERTS * S - S)
                    sp.dma_start(xt[m][:], xs[bass.ds(first, S)]).then_inc(xt_in[m], 16)
                if store:
                    sp.wait_ge(y_ready, LEAD + n - 3)
                    carry_wait(sp)
                    first = sp.value_load(tile_row[0:1, bass.ds(i + m - 4, 1)], min_val=0, max_val=EXPERTS * R + EXPERTS * S - S)
                    sp.dma_start(ys[bass.ds(first, S)], y[m][:]).then_inc(y_stored[m], 16)

            def combine(o):
                sp.wait_ge(out_stored, LEAD + 16 * o)
                sp.dma_start(h_back[:], hmid.rearrange("(o j) s d -> o s j d", j=OB)[o]).then_inc(h_in, 16)
                sp.wait_ge(total_ready, LEAD + 2 * (o + 1))
                sp.dma_start(out.rearrange("(o j) s d -> o s j d", j=OB)[o], h_back[:]).then_inc(out_stored, 16)

            load_codes(0, 0)
            load_codes(1, 1)
            sp.wait_ge(s_yzero, 16 * (EXPERTS + 1))
            with sp.Fori(0, chunks) as c:
                octet(c * per_chunk, octet_steps(False))
                if per_chunk > 1:
                    with sp.Fori(1, per_chunk) as i:
                        octet(c * per_chunk + i, octet_steps(True))
                octet(c * per_chunk + per_chunk - 1, last_steps())
                pad(c)
                for m in range(4):
                    tile(c, 0, m, store=False)
                with sp.Fori(1, TILES // 4) as q:
                    for m in range(4):
                        tile(c, q, m)
                for m in range(4):
                    tile(c, TILES // 4, m, load=False)
                for par in range(2):
                    sp.wait_ge(h2_stored[par], LEAD + 16 * per_chunk * (c + 1))
                carry_wait(sp)
                with sp.Fori(0, per_chunk) as i:
                    combine(c * per_chunk + i)
            sp.wait_ge(out_stored, LEAD + 16 * octets)

        @block.gpsimd
        def _(pool):
            own = [0]

            def link(ins):
                own[0] += 1
                ins.then_inc(p_own, 1)
                pool.wait_ge(p_own, own[0])

            link(pool.memset(ident[:], 0.0))
            link(pool.affine_select(out=ident[:], in_=ident[:], compare_op=ALU.not_equal, fill=1.0, base=0,
                                    pattern=[[-1, 128]], channel_multiplier=1))
            link(pool.memset(causal[:], HUGE))
            link(pool.affine_select(out=causal[:], in_=causal[:], compare_op=ALU.is_ge, fill=NEG_INF, base=0,
                                    pattern=[[-1, 128]], channel_multiplier=1))
            link(pool.memset(ones[:], 1.0))
            link(pool.memset(earlier[:], 1.0))
            link(pool.affine_select(out=earlier[:], in_=earlier[:], compare_op=ALU.is_gt, fill=0.0, base=0,
                                    pattern=[[1, 128]], channel_multiplier=-1))
            link(pool.iota(expert_no[:], pattern=[[1, EXPERTS]], base=0, channel_multiplier=0,
                      allow_small_or_imprecise_dtypes=True))
            link(pool.iota(region[:], pattern=[[R, EXPERTS]], base=0, channel_multiplier=0,
                      allow_small_or_imprecise_dtypes=True))
            link(pool.iota(tile_no[:], pattern=[[1, TILES]], base=0, channel_multiplier=0,
                      allow_small_or_imprecise_dtypes=True))
            pool.memset(zeros[:], 0.0).then_inc(s_zero, 1)
            pool.memset(minus_half[:], -0.5).then_inc(s_pool, 1)
            pool.iota(small[:, 0:1], pattern=[[0, 1]], base=0, channel_multiplier=1,
                      allow_small_or_imprecise_dtypes=True).then_inc(s_const, 1)

            def step(o, st):
                kind, i = st[0], st[1]
                if kind == "embed":
                    G = 2 * o + i
                    pool.wait_ge(moments_ready, LEAD + G + 1)
                    pool.wait_ge(normed_ready, LEAD + G)
                    carry_wait(pool)
                    pool.tensor_scalar(var_eps[:], moments[:, :, 1], EPS, None, ALU.add).then_inc(var_ready, 1)
                    pool.wait_ge(var_ready, LEAD + G + 1)
                    pool.tensor_tensor(rstd[:], var_eps[:], minus_half[:], ALU.pow).then_inc(rstd_ready, 1)
                elif kind == "route_norm":
                    G = 2 * o + i
                    pool.wait_ge(moments2_ready, LEAD + G + 1)
                    pool.wait_ge(normed2_ready, LEAD + G)
                    carry_wait(pool)
                    pool.tensor_scalar(var_eps2[:], moments2[:, :, 1], EPS, None, ALU.add).then_inc(var2_ready, 1)
                    pool.wait_ge(var2_ready, LEAD + G + 1)
                    pool.tensor_tensor(rstd2[:], var_eps2[:], minus_half[:], ALU.pow).then_inc(rstd2_ready, 1)
                elif kind == "residual":
                    G = 2 * o + i
                    pool.wait_ge(embedded, LEAD + G + 1)
                    pool.wait_ge(h2_ready, LEAD + GB * (G - 1))
                    pool.tensor_tensor(residual[i % 2][:], h[i % 2][:], bias_o[:].unsqueeze(1).broadcast_to([S, GB, D]),
                                       ALU.add).then_inc(residual_ready, 1)
                elif kind == "route_choose":
                    G = 2 * o + i
                    pool.wait_ge(chosen_ready, LEAD + 2 * (G + 1))
                    pool.wait_ge(ranks_full, LEAD + G)
                    pool.tensor_tensor(picked[:], chosen[:, 0], chosen[:, 1], ALU.add).then_inc(picked_ready, 1)
                elif kind == "route_ranks":
                    G = 2 * o + i
                    pool.wait_ge(ranks_ready, LEAD + G + 1)
                    for j in range(GB):
                        pool.tensor_tensor(filled[:, j + 1], filled[:, j], ranks[:, 1, j], ALU.add).then_inc(filled_step, 1)
                        pool.wait_ge(filled_step, LEAD + GB * G + j + 1)
                    pool.tensor_tensor(rows_f[:], ranks[:, 0], filled[:, 0:GB], ALU.add).then_inc(rows_c, 1)
                    pool.wait_ge(rows_c, LEAD + G + 1)
                    for k in range(2):
                        pool.tensor_tensor(rows_2[:, k], rows_f[:], chosen[:, k], ALU.mult).then_inc(rows_a, 1)
                    pool.tensor_copy(filled[:, 0], filled[:, GB]).then_inc(filled_next, 1)
                elif kind == "route_rows":
                    G, par = 2 * o + i, i % 2
                    pool.wait_ge(row_ready, LEAD + G + 1)
                    carry_wait(pool)
                    pool.tensor_copy(rows_all[:, :, bass.ds(place(o, i), GB)], row[par][:]).then_inc(rows_kept, 1)
                elif kind == "scatter":
                    par, k = i % 2, st[2]
                    for j in range(GB):
                        pool.indirect_dma_start(xs, bass.IndirectOffsetOnAxis(ap=row[par][:, k, j:j + 1].bitcast(U32), axis=0),
                                                normed2[par][:, j], None).then_inc(scattered[par], 16)
                elif kind == "route_weight":
                    G = 2 * o + i
                    pool.wait_ge(weight1_ready, LEAD + G + 1)
                    carry_wait(pool)
                    pool.tensor_copy(weights_all[:, :, bass.ds(place(o, i), GB)], weight[:]).then_inc(weights_kept, 1)

            def place(o, i):
                return (2 * local[0] + i) * GB

            local = [0]

            pool.wait_ge(s_zero, 1)
            for n, s in enumerate(scattered + [y_in]):
                pool.dma_start(spare[n:n + 1], zeros[0:1]).then_inc(s, SW_LEAD)
            pool.wait_ge(s_wqkv, 16 * 8)
            pool.wait_ge(s_pool, 1)
            for st in first_steps():
                step(0, st)
            with pool.Fori(0, chunks) as c:
                pool.wait_ge(table_ready, LEAD + 2 * c)
                pool.wait_ge(filled_next, LEAD + 2 * per_chunk * c)
                pool.wait_ge(ends_ready, LEAD + c)
                carry_wait(pool)
                pool.tensor_copy(filled[:, 0], region[:]).then_inc(filled_start, 1)
                pool.wait_ge(filled_start, LEAD + c + 1)
                local[0] = 0
                for st in octet_steps(False):
                    step(c * per_chunk, st)
                if per_chunk > 1:
                    with pool.Fori(1, per_chunk) as i:
                        local[0] = i
                        for st in octet_steps(True):
                            step(c * per_chunk + i, st)
                local[0] = per_chunk - 1
                for st in last_steps():
                    step(c * per_chunk + per_chunk - 1, st)
                pool.wait_ge(filled_next, LEAD + 2 * per_chunk * (c + 1))
                carry_wait(pool)
                pool.tensor_copy(ends[:], filled[0:1, 0]).then_inc(ends_ready, 1)
                for m in range(4):
                    pool.wait_ge(y_stored[m], LEAD + 16 * (TILES // 4) * (c + 1))
                carry_wait(pool)
                with pool.Fori(0, per_chunk) as i:
                    o = c * per_chunk + i
                    pool.wait_ge(y_in, SW_LEAD + 16 * 2 * OB * o)
                    carry_wait(pool)
                    pool.tensor_copy(rows_now[:], rows_all[:, :, bass.ds(i * OB, OB)]).then_inc(rows_now_ready, 1)
                    pool.wait_ge(total_ready, LEAD + 2 * o)
                    pool.wait_ge(rows_now_ready, LEAD + o + 1)
                    carry_wait(pool)
                    pool.tensor_copy(weights_now[:], weights_all[:, :, bass.ds(i * OB, OB)]).then_inc(weights_now_ready, 1)
                    for j in range(OB):
                        for k in range(2):
                            pool.indirect_dma_start(y_rows[:, k, j], None, ys,
                                                    bass.IndirectOffsetOnAxis(ap=rows_now[:, k, j:j + 1].bitcast(U32), axis=0)).then_inc(y_in, 16)

        @block.scalar
        def _(act):
            act.wait_ge(s_zero, 1)
            for n in range(EXPERTS):
                act.dma_start(ys[n * R:(n + 1) * R].rearrange("(p r) d -> p r d", p=S),
                              zeros[:].unsqueeze(1).broadcast_to([S, R // S, D])).then_inc(s_yzero, 16)
            act.dma_start(ys[EXPERTS * R:].rearrange("(p r) d -> p r d", p=S),
                          zeros[:].unsqueeze(1).broadcast_to([S, EXPERTS, D])).then_inc(s_yzero, 16)
            act.wait_ge(s_wqkv, 16 * 8)
            nc.scalar.mul(bias_q8[:], bias_qk[:, 0], HD ** -0.5).then_inc(s_whi, 1)
            nc.scalar.copy(w_hi[:], w_raw[:]).then_inc(s_whi, 1)
            act.wait_ge(s_whi, 2)
            act.wait_ge(s_w1, 16 * 5)
            for n in range(2):
                nc.scalar.copy(w1_hi[:, n * EXPERTS * FC1 // 2:(n + 1) * EXPERTS * FC1 // 2],
                               w1_raw[n][:].rearrange("p a b -> p (a b)")).then_inc(s_w1hi, 1)
            act.wait_ge(s_w1lo, 2)

            def tile(c, q, m, kinds):
                i = 4 * q
                n = c * TILES + i
                if "x" in kinds:
                    k, par = n + m, m % 2
                    act.wait_ge(x3T_full, LEAD + k + 1)
                    act.wait_ge(fc1_full, LEAD + k - 1)
                    nc.scalar.copy(x3_hi[par][:], ps[:, XB + par, 0:S]).then_inc(x3hi_ready, 1)
                if "h" in kinds:
                    k, par = n + m - 1, (m - 1) % 2
                    act.wait_ge(fc1_full, LEAD + k + 1)
                    act.wait_ge(act_ready, LEAD + k - 1)
                    nc.scalar.activation(gate[par][:], ps[:, HB + par, 0:HID], ACT.Silu).then_inc(gate_ready, 1)
                if "y" in kinds:
                    k, par, slot = n + m - 3, (m - 3) % 2, (m - 3) % 4
                    act.wait_ge(fc2_full, LEAD + k + 1)
                    turn = c * (TILES // 4) + (q if m == 3 else q - 1)
                    act.wait_ge(y_stored[slot], LEAD + 16 * turn)
                    nc.scalar.copy(y[slot][:], ps[:, YB + par, 0:D]).then_inc(y_ready, 1)

            def step(o, st):
                kind, i = st[0], st[1]
                if kind == "normT":
                    G, par = 2 * o + i, i % 2
                    act.wait_ge(normT_full, LEAD + G + 1)
                    act.wait_ge(v_full, LEAD + GB * (G - 1))
                    act.wait_ge(qk_full, LEAD + 2 * PAIRS * (G - 1))
                    nc.scalar.copy(xT_hi[par][:], ps[:, ROT]).then_inc(xhi_ready, 1)
                elif kind in ("query", "key"):
                    G, par, pair = 2 * o + i, i % 2, st[2]
                    n = 2 * pair + (kind == "key")
                    act.wait_ge(qk_full, LEAD + 2 * PAIRS * G + n + 1)
                    if n == 0:
                        act.wait_ge(scores_full, LEAD + GB * (G - 1))
                    if kind == "query":
                        nc.scalar.activation(qT[par][:, pair], ps[:, QK], ACT.Identity, bias=bias_q8[:, pair:pair + 1],
                                             scale=HD ** -0.5).then_inc(qk_ready, 1)
                    else:
                        nc.scalar.activation(kT[par][:, pair], ps[:, QK], ACT.Identity, bias=bias_qk[:, 1, pair:pair + 1],
                                             scale=1.0).then_inc(qk_ready, 1)
                elif kind == "exp":
                    b, par, half = OB * o + i, i % 2, st[2]
                    if half == 0:
                        act.wait_ge(max_ready, LEAD + b + 1)
                        act.wait_ge(pTb_full, LEAD + b - 1)
                        act.wait_ge(mixed_ready, LEAD + b - 1)
                    for n in range(half * PAIRS, (half + 1) * PAIRS):
                        ins = nc.scalar.activation(probs[par][:, n], masked[par][:, n], ACT.Exp, bias=neg_max[par][:, n:n + 1],
                                                   scale=1.0, accum_out=sums[par][:, n:n + 1])
                    if half == 1:
                        ins.then_inc(probs_ready, 1)
                elif kind == "probsT":
                    b = OB * o + i
                    act.wait_ge(pTa_full, LEAD + b + 1)
                    act.wait_ge(mix_full, LEAD + b)
                    nc.scalar.copy(probsT[:, 0:4], ps[:, PROBST]).then_inc(pTa_ready, 1)
                elif kind == "route_ranks":
                    G = 2 * o + i
                    act.wait_ge(gap_ready, LEAD + G + 1)
                    act.wait_ge(weight1_ready, LEAD + G)
                    nc.scalar.activation(gap_exp[:], gap[:], ACT.Exp).then_inc(gap_exp_ready, 1)
                elif kind == "mixT":
                    b = OB * o + i
                    act.wait_ge(mixT_full, LEAD + b + 1)
                    act.wait_ge(project_full, LEAD + b)
                    nc.scalar.copy(mixedT[:], ps[:, MIXT]).then_inc(mixT_ready, 1)

            for st in first_steps():
                step(0, st)
            with act.Fori(0, chunks) as c:
                for st in octet_steps(False):
                    step(c * per_chunk, st)
                if per_chunk > 1:
                    with act.Fori(1, per_chunk) as i:
                        for st in octet_steps(True):
                            step(c * per_chunk + i, st)
                for st in last_steps():
                    step(c * per_chunk + per_chunk - 1, st)
                each_tile(act, c, tile, ("x", "h", "y"), (0, 1, 3))

        @block.vector
        def _(dve):
            own = [0]

            def link(ins):
                own[0] += 1
                ins.then_inc(s_dve, 1)
                dve.wait_ge(s_dve, own[0])

            V = nc.vector
            dve.wait_ge(s_x, 16)
            xf, up, down, gt = scan
            link(V.tensor_copy(xf[:], x_raw[:]))
            link(V.tensor_scalar(gt[:], xf[:], 39990.0, None, ALU.is_gt))
            link(V.tensor_scalar(up[:], xf[:], 40.0, None, ALU.is_equal))
            link(V.tensor_scalar(down[:], xf[:], 41.0, None, ALU.is_equal))
            for o_, c_ in ((123.0, 125.0), (91.0, 93.0)):
                link(V.scalar_tensor_tensor(up[:], xf[:], o_, up[:], ALU.is_equal, ALU.add))
                link(V.scalar_tensor_tensor(down[:], xf[:], c_, down[:], ALU.is_equal, ALU.add))
            link(V.tensor_tensor(up[:], up[:], down[:], ALU.subtract))
            link(V.memset(xf[:], 0.0))
            link(V.tensor_tensor_scan(down[:], up[:], xf[:], 0.0, ALU.add, ALU.add))
            link(V.tensor_tensor_scan(up[:], gt[:], xf[:], 0.0, ALU.add, ALU.add))
            link(V.tensor_copy(seg_int[:], up[:]))
            link(V.tensor_tensor_scan(gt[:], down[:], down[:], 0.0, ALU.min, ALU.min))
            link(V.tensor_tensor(down[:], down[:], gt[:], ALU.subtract))
            V.tensor_scalar(codes_sb[:, 0], down[:], 0.0, float(NEST - 1), ALU.max, ALU.min).then_inc(s_codes, 1)
            link(V.tensor_scalar(seg_int[:], seg_int[:], SEG - 1, None, ALU.bitwise_and))
            V.tensor_copy(codes_sb[:, 1], seg_int[:]).then_inc(s_codes, 1)
            dve.wait_ge(s_const, 1)
            p = small[:, 0:1]
            acc, cmp_ = small[:, 1:2], small[:, 2:3]
            n3 = PARTS * NEST
            link(V.tensor_copy(part_code[:], p))
            link(V.memset(acc, 0.0))
            for edge, code_step, part_step in ((NEST, -NEST, 1), (2 * NEST, -NEST, 1), (n3, -NEST, -2),
                                               (n3 + SEG, -SEG, 1), (n3 + 2 * SEG, -SEG, 1)):
                link(V.tensor_scalar(cmp_, p, float(edge), None, ALU.is_ge))
                link(V.scalar_tensor_tensor(part_code[:], cmp_, float(code_step), part_code[:], ALU.mult, ALU.add))
                link(V.scalar_tensor_tensor(acc, cmp_, float(part_step), acc, ALU.mult, ALU.add))
            for n in range(PARTS):
                link(V.tensor_scalar(part_mask[:, n:n + 1], acc, float(n), None, ALU.is_equal))
            dve.wait_ge(s_table_ps, 1)
            link(V.tensor_copy(pos_emb[:], ps[:, ROT, 0:D]))
            link(V.tensor_copy(t_full[:], ps[0:CODES, ROT, D:2 * D]))
            link(V.tensor_copy(t_hi[:], t_full[:]))
            link(V.tensor_tensor(t_rest[:], t_full[:], t_hi[:], ALU.subtract))
            link(V.tensor_copy(t_mid[:], t_rest[:]))
            link(V.tensor_tensor(t_rest2[:], t_rest[:], t_mid[:], ALU.subtract))
            link(V.tensor_copy(t_lo[:], t_rest2[:]))
            link(V.tensor_scalar(t_acc[:], t_hi[:], part_mask[:, 0:1], None, ALU.mult))
            link(V.scalar_tensor_tensor(t_acc[:], t_mid[:], part_mask[:, 1:2], t_acc[:], ALU.mult, ALU.add))
            V.scalar_tensor_tensor(code_table[:], t_lo[:], part_mask[:, 2:3], t_acc[:], ALU.mult, ALU.add).then_inc(s_table, 1)
            dve.wait_ge(s_whi, 2)
            V.tensor_tensor(w_lo[:], w_raw[:], w_hi[:].bitcast(F32), ALU.subtract).then_inc(s_wlo, 1)
            for n in range(2):
                dve.wait_ge(s_w1hi, n + 1)
                cols = slice(n * EXPERTS * FC1 // 2, (n + 1) * EXPERTS * FC1 // 2)
                V.tensor_tensor(w1_lo[:, cols], w1_raw[n][:].rearrange("p a b -> p (a b)"), w1_hi[:, cols].bitcast(F32),
                                ALU.subtract).then_inc(s_w1lo, 1)
            dve.wait_ge(s_bias, 16 * 2 * PARTS)
            nb = PARTS * EXPERTS
            link(V.tensor_scalar(small[0:nb, 1:2], small[0:nb, 0:1], float(EXPERTS), None, ALU.is_ge))
            link(V.tensor_scalar(small[0:nb, 2:3], small[0:nb, 0:1], float(2 * EXPERTS), None, ALU.is_ge))
            link(V.tensor_tensor(small[0:nb, 3:4], small[0:nb, 1:2], small[0:nb, 2:3], ALU.add))
            for n in range(PARTS):
                link(V.tensor_scalar(b_mask[:, n:n + 1], small[0:nb, 3:4], float(n), None, ALU.is_equal))
            link(V.tensor_copy(b_hi[:], b12[:]))
            link(V.tensor_tensor(b_rest[:], b12[:], b_hi[:], ALU.subtract))
            link(V.tensor_copy(b_mid[:], b_rest[:]))
            link(V.tensor_tensor(b_rest[:], b_rest[:], b_mid[:], ALU.subtract))
            link(V.tensor_scalar(b_rest[:], b_rest[:], b_mask[:, 2:3], None, ALU.mult))
            link(V.scalar_tensor_tensor(b_rest[:], b_mid[:], b_mask[:, 1:2], b_rest[:], ALU.mult, ALU.add))
            V.scalar_tensor_tensor(b_parts[:], b_hi[:], b_mask[:, 0:1], b_rest[:], ALU.mult, ALU.add).then_inc(s_bparts, 1)
            dve.wait_ge(s_table, 1)
            dve.wait_ge(s_pool, 1)

            def step(o, st):
                kind, i = st[0], st[1]
                G, b, par = 2 * o + i, OB * o + i, i % 2
                if kind == "onehot":
                    dve.wait_ge(codes_in[par], LEAD + 16 * (G - par + 2))
                    dve.wait_ge(embed_full, LEAD + G)
                    V.tensor_scalar(onehot[:], code_rows[par][:], part_code[:], None, ALU.is_equal).then_inc(onehot_ready, 1)
                elif kind == "embed":
                    dve.wait_ge(embed_full, LEAD + G + 1)
                    dve.wait_ge(residual_ready, LEAD + G - 1)
                    V.tensor_tensor(h[par][:], ps[:, ROT].rearrange("p (j d) -> p j d", j=GB),
                                    pos_emb[:].unsqueeze(1).broadcast_to([S, GB, D]), ALU.add).then_inc(embedded, 1)
                    dve.wait_ge(embedded, LEAD + G + 1)
                    dve.wait_ge(normed_ready, LEAD + G)
                    for j in range(GB):
                        ins = V.bn_stats(stats[:, j], h[par][:, j])
                    ins.then_inc(bn_done, 1)
                    dve.wait_ge(bn_done, LEAD + G + 1)
                    carry_wait(dve)
                    for j in range(GB):
                        ins = V.bn_aggr(moments[:, j], stats[:, j])
                    ins.then_inc(moments_ready, 1)
                elif kind == "norm":
                    dve.wait_ge(rstd_ready, LEAD + G + 1)
                    dve.wait_ge(normT_full, LEAD + G)
                    for j in range(GB):
                        ins = V.tensor_scalar(normed[:, j], h[par][:, j], moments[:, j, 0:1], rstd[:, j:j + 1],
                                              ALU.subtract, ALU.mult)
                    ins.then_inc(normed_ready, 1)
                elif kind == "normT":
                    dve.wait_ge(xhi_ready, LEAD + G + 1)
                    V.tensor_tensor(xT_lo[par][:], ps[:, ROT], xT_hi[par][:].bitcast(F32), ALU.subtract).then_inc(xlo_ready, 1)
                elif kind == "value":
                    j = st[2]
                    dve.wait_ge(v_full, LEAD + GB * G + j + 1)
                    if j == 0:
                        dve.wait_ge(mix_full, LEAD + GB * (G - 1))
                    V.tensor_tensor(v[par][:, j], ps[:, ROT], bias_v[:], ALU.add).then_inc(v_ready, 1)
                elif kind == "scores":
                    dve.wait_ge(scores_full, LEAD + b + 1)
                    dve.wait_ge(probs_ready, LEAD + b - 1)
                    V.tensor_tensor(masked[par][:], ps[:, SCORES:SCORES + 2].rearrange("p a (n k) -> p (a n) k", n=4),
                                    causal[:].unsqueeze(1).broadcast_to([S, HEADS, S]), ALU.min).then_inc(masked_ready, 1)
                elif kind == "max":
                    dve.wait_ge(masked_ready, LEAD + b + 1)
                    V.tensor_reduce(neg_max[par][:], masked[par][:], AX, ALU.max, negate=True).then_inc(max_ready, 1)
                elif kind == "probsT":
                    dve.wait_ge(pTb_full, LEAD + b + 1)
                    dve.wait_ge(mix_full, LEAD + b)
                    V.tensor_copy(probsT[:, 4:8], ps[:, PROBST + 1].rearrange("p (n k) -> p n k", n=4)).then_inc(pTb_ready, 1)
                    dve.wait_ge(probs_ready, LEAD + b + 1)
                    V.reciprocal(inv_sums[:], sums[par][:]).then_inc(inv_ready, 1)
                elif kind == "mix":
                    dve.wait_ge(inv_ready, LEAD + b + 1)
                    dve.wait_ge(mix_full, LEAD + b + 1)
                    dve.wait_ge(mixT_full, LEAD + b)
                    V.tensor_tensor(mixed[:].rearrange("p (m e d) -> p e m d", e=2, d=HD),
                                    ps[:, MIX].rearrange("p (m e d) -> p e m d", e=2, d=HD),
                                    inv_sums[:].rearrange("p (e m) -> p e m", e=2).unsqueeze(3).broadcast_to([S, 2, PAIRS, HD]),
                                    ALU.mult).then_inc(mixed_ready, 1)
                elif kind == "project":
                    j, hp = i % GB, (i // GB) % 2
                    dve.wait_ge(project_full, LEAD + b + 1)
                    if j == 0:
                        dve.wait_ge(h2_stored[hp], LEAD + 16 * group_turn(o, i))
                    if j == 0:
                        dve.wait_ge(residual_ready, LEAD + 2 * o + (i // GB) + 1)
                        dve.wait_ge(normed2_ready, LEAD + 2 * o + (i // GB) - 1)
                    V.tensor_tensor(h2[hp][:, j], ps[:, ROT, 0:D], residual[hp][:, j], ALU.add).then_inc(h2_ready, 1)
                elif kind == "route_norm":
                    dve.wait_ge(h2_ready, LEAD + GB * (G + 1))
                    dve.wait_ge(moments2_ready, LEAD + G)
                    for j in range(GB):
                        ins = V.bn_stats(stats2[:, j], h2[par][:, j])
                    ins.then_inc(bn2_done, 1)
                    dve.wait_ge(bn2_done, LEAD + G + 1)
                    dve.wait_ge(normed2_ready, LEAD + G)
                    carry_wait(dve)
                    for j in range(GB):
                        ins = V.bn_aggr(moments2[:, j], stats2[:, j])
                    ins.then_inc(moments2_ready, 1)
                elif kind == "route_scale":
                    dve.wait_ge(rstd2_ready, LEAD + G + 1)
                    dve.wait_ge(scattered[par], SW_LEAD + 16 * 2 * GB * (o + (i - par) // 2))
                    dve.wait_ge(x2T_full, LEAD + G - 1)
                    for j in range(GB):
                        ins = V.tensor_scalar(normed2[par][:, j], h2[par][:, j], moments2[:, j, 0:1], rstd2[:, j:j + 1],
                                              ALU.subtract, ALU.mult)
                    ins.then_inc(normed2_ready, 1)
                elif kind == "route_normT":
                    dve.wait_ge(x2T_full, LEAD + G + 1)
                    dve.wait_ge(logits_full, LEAD + G)
                    V.tensor_copy(x2T[:], ps[:, ROT]).then_inc(x2T_ready, 1)
                elif kind == "route_logits":
                    dve.wait_ge(logits_full, LEAD + G + 1)
                    dve.wait_ge(top_at_ready, LEAD + G)
                    V.tensor_tensor(logits[:], ps[:, ROT, 0:GB * EXPERTS].rearrange("p (j e) -> p j e", j=GB),
                                    bias_r[:].unsqueeze(1).broadcast_to([S, GB, EXPERTS]), ALU.add).then_inc(logits_ready, 1)
                    dve.wait_ge(logits_ready, LEAD + G + 1)
                    dve.wait_ge(gap_ready, LEAD + G)
                    carry_wait(dve)
                    for j in range(GB):
                        ins = V.max(top[:, j], logits[:, j])
                    ins.then_inc(top_ready, 1)
                    dve.wait_ge(top_ready, LEAD + G + 1)
                    dve.wait_ge(top_no_ready, LEAD + G)
                    carry_wait(dve)
                    for j in range(GB):
                        ins = V.max_index(top_at[:, j], top[:, j], logits[:, j])
                    ins.then_inc(top_at_ready, 1)
                elif kind == "route_choose":
                    dve.wait_ge(gap_exp_ready, LEAD + G)
                    V.tensor_tensor(gap[:], top[:, :, 1], top[:, :, 0], ALU.subtract).then_inc(gap_ready, 1)
                    dve.wait_ge(top_at_ready, LEAD + G + 1)
                    dve.wait_ge(chosen_ready, LEAD + 2 * G)
                    V.tensor_copy(top_no[:], top_at[:, :, 0:2]).then_inc(top_no_ready, 1)
                    dve.wait_ge(top_no_ready, LEAD + G + 1)
                    dve.wait_ge(picked_ready, LEAD + G)
                    dve.wait_ge(rows_a, LEAD + 2 * G)
                    for k in range(2):
                        V.tensor_tensor(chosen[:, k], expert_no[:].unsqueeze(1).broadcast_to([S, GB, EXPERTS]),
                                        top_no[:, :, k:k + 1].broadcast_to([S, GB, EXPERTS]), ALU.is_equal).then_inc(chosen_ready, 1)
                elif kind == "route_weight":
                    dve.wait_ge(gap_exp_ready, LEAD + G + 1)
                    V.tensor_scalar(gap_one[:], gap_exp[:], 1.0, None, ALU.add).then_inc(gap_one_ready, 1)
                    dve.wait_ge(gap_one_ready, LEAD + G + 1)
                    dve.wait_ge(weights_kept, LEAD + G)
                    V.reciprocal(weight[:, 0], gap_one[:]).then_inc(weight0_ready, 1)
                    dve.wait_ge(weight0_ready, LEAD + G + 1)
                    V.tensor_tensor(weight[:, 1], gap_exp[:], weight[:, 0], ALU.mult).then_inc(weight1_ready, 1)
                elif kind == "route_ranks":
                    dve.wait_ge(ranks_full, LEAD + G + 1)
                    dve.wait_ge(rows_c, LEAD + G)
                    V.tensor_copy(ranks[:], ps[:, ROT, 0:2 * GB * EXPERTS].rearrange("p (a j e) -> p a j e", a=2, j=GB)).then_inc(ranks_ready, 1)
                elif kind == "route_rows":
                    dve.wait_ge(rows_a, LEAD + 2 * (G + 1))
                    dve.wait_ge(row_ready, LEAD + G)
                    V.tensor_reduce(row_f[:], rows_2[:], AX, ALU.add).then_inc(rows_b, 1)
                    dve.wait_ge(rows_b, LEAD + G + 1)
                    dve.wait_ge(scattered[par], SW_LEAD + 16 * 2 * GB * (o + (i - par) // 2))
                    dve.wait_ge(rows_kept, LEAD + G - 1)
                    V.tensor_copy(row[par][:], row_f[:]).then_inc(row_ready, 1)

            def group_turn(o, i):
                return o + (0 if i >= 0 else -1)

            def table(c):
                dve.wait_ge(ends_ready, LEAD + c + 1)
                n = [0]

                def link(ins):
                    n[0] += 1
                    ins.then_inc(table_own, 1)
                    dve.wait_ge(table_own, LEAD + c * TABLE_STEPS + n[0])

                link(V.tensor_copy(tiles_f[:], ends[:]))
                link(V.tensor_tensor(tiles_f[:], tiles_f[:], region[0:1], ALU.subtract))
                link(V.tensor_scalar(tiles_i[:], tiles_f[:], float(S - 1), None, ALU.add))
                link(V.tensor_scalar(tiles_i[:], tiles_i[:], 7, None, ALU.logical_shift_right))
                link(V.tensor_copy(tiles_f[:], tiles_i[:]))
                link(V.tensor_tensor_scan(tiles_end[:], tiles_f[:], tab[:, 3, 0:EXPERTS], 0.0, ALU.add, ALU.add))
                link(V.tensor_tensor(passed[:], tile_no[:].unsqueeze(2).broadcast_to([1, TILES, EXPERTS]),
                                     tiles_end[:].unsqueeze(1).broadcast_to([1, TILES, EXPERTS]), ALU.is_ge))
                link(V.tensor_reduce(tab[:, 0], passed[:], AX, ALU.add))
                link(V.tensor_tensor(passed[:], passed[:], tiles_f[:].unsqueeze(1).broadcast_to([1, TILES, EXPERTS]), ALU.mult))
                link(V.tensor_reduce(tab[:, 1], passed[:], AX, ALU.add))
                link(V.tensor_tensor(tab[:, 1], tile_no[:], tab[:, 1], ALU.subtract))
                link(V.tensor_scalar(tab[:, 1], tab[:, 1], float(S), None, ALU.mult))
                link(V.scalar_tensor_tensor(tab[:, 1], tab[:, 0], float(R), tab[:, 1], ALU.mult, ALU.add))
                assert n[0] == TABLE_STEPS
                V.tensor_copy(tile_row[:], tab[:, 1]).then_inc(table_ready, 1)
                V.tensor_scalar(tile_expert[:], tab[:, 0], float(EXPERTS - 1), None, ALU.min).then_inc(table_ready, 1)

            def tile(c, q, m, kinds):
                i = 4 * q
                n = c * TILES + i
                if "x" in kinds:
                    k, par = n + m, m % 2
                    dve.wait_ge(x3hi_ready, LEAD + k + 1)
                    V.tensor_tensor(x3_lo[par][:], ps[:, XB + par, 0:S], x3_hi[par][:].bitcast(F32), ALU.subtract).then_inc(x3lo_ready, 1)
                if "h" in kinds:
                    k, par = n + m - 1, (m - 1) % 2
                    dve.wait_ge(gate_ready, LEAD + k + 1)
                    dve.wait_ge(actT_full, LEAD + k - 1)
                    V.tensor_tensor(act_out[par][:], gate[par][:], ps[:, HB + par, HID:FC1], ALU.mult).then_inc(act_ready, 1)
                if "a" in kinds:
                    k, par = n + m - 2, m % 2
                    dve.wait_ge(actT_full, LEAD + k + 1)
                    dve.wait_ge(fc2_full, LEAD + k - 1)
                    V.tensor_copy(actT[par][:], ps[:, AB + par, 0:HID].rearrange("p (a s) -> p a s", a=2)).then_inc(actT_ready, 1)

            link(V.memset(tab[:, 3], 0.0))
            for st in first_steps():
                step(0, st)
            with dve.Fori(0, chunks) as c:
                for st in octet_steps(False):
                    step(c * per_chunk, st)
                if per_chunk > 1:
                    with dve.Fori(1, per_chunk) as i:
                        for st in octet_steps(True):
                            step(c * per_chunk + i, st)
                for st in last_steps():
                    step(c * per_chunk + per_chunk - 1, st)
                table(c)
                each_tile(dve, c, tile, ("x", "h", "a"), (0, 1, 2))
                with dve.Fori(0, per_chunk) as i:
                    o = c * per_chunk + i
                    dve.wait_ge(y_in, SW_LEAD + 16 * 2 * OB * (o + 1))
                    dve.wait_ge(h_in, LEAD + 16 * (o + 1))
                    dve.wait_ge(weights_now_ready, LEAD + o + 1)
                    for k in range(2):
                        for j in range(OB):
                            ins = V.scalar_tensor_tensor(h_back[:, j], y_rows[:, k, j], weights_now[:, k, j:j + 1],
                                                         h_back[:, j], ALU.mult, ALU.add)
                        ins.then_inc(total_ready, 1)
                        dve.wait_ge(total_ready, LEAD + 2 * o + k + 1)

        @block.tensor
        def _(pe):
            T = nc.tensor
            pe.wait_ge(s_w, 16 * 4)
            T.matmul(ps[:, ROT, 0:D], posT[:], w_emb[:, 0], start=True, stop=True, skip_group_check=True)
            T.matmul(ps[0:CODES, ROT, D:2 * D], nestT[:], w_emb[:, 1], start=False, stop=False, skip_group_check=True)
            T.matmul(ps[0:CODES, ROT, D:2 * D], segT[:], w_emb[:, 2], start=False, stop=True, skip_group_check=True).then_inc(s_table_ps, 1)
            pe.wait_ge(s_table, 1)
            pe.wait_ge(s_wlo, 1)
            pe.wait_ge(s_pool, 1)

            def three(dst, w_hi_, w_lo_, x_hi_, x_lo_):
                T.matmul(dst, w_hi_, x_hi_, start=True, stop=False)
                T.matmul(dst, w_hi_, x_lo_, start=False, stop=False)
                return T.matmul(dst, w_lo_, x_hi_, start=False, stop=True)

            rot_free = {}

            def step(o, st, last_rot):
                kind, i = st[0], st[1]
                G, b, par = 2 * o + i, OB * o + i, i % 2

                def wait_rot():
                    k, n = last_rot[0], last_rot[1]
                    if k == "embed":
                        pe.wait_ge(embedded, LEAD + 2 * o + n + 1)
                    elif k == "normT":
                        pe.wait_ge(xlo_ready, LEAD + 2 * o + n + 1)
                    elif k == "value":
                        pe.wait_ge(v_ready, LEAD + GB * (2 * o + n) + last_rot[2] + 1)
                    elif k == "project":
                        pe.wait_ge(h2_ready, LEAD + OB * o + n + 1)
                    elif k == "route_normT":
                        pe.wait_ge(x2T_ready, LEAD + 2 * o + n + 1)
                    elif k == "route_logits":
                        pe.wait_ge(logits_ready, LEAD + 2 * o + n + 1)
                    elif k == "route_ranks":
                        pe.wait_ge(ranks_ready, LEAD + 2 * o + n + 1)

                if kind == "embed":
                    wait_rot()
                    pe.wait_ge(onehot_ready, LEAD + G + 1)
                    for j in range(GB):
                        ins = T.matmul(ps[:, ROT, j * D:(j + 1) * D], onehot[:, j * S:(j + 1) * S], code_table[:],
                                       start=True, stop=True)
                    ins.then_inc(embed_full, 1)
                elif kind == "normT":
                    wait_rot()
                    pe.wait_ge(normed_ready, LEAD + G + 1)
                    for j in range(GB):
                        ins = T.transpose(ps[:, ROT, j * S:(j + 1) * S], normed[:, j], ident[:])
                    ins.then_inc(normT_full, 1)
                elif kind in ("query", "key"):
                    pair = st[2]
                    n = 2 * pair + (kind == "key")
                    w = int(kind == "key")
                    if n == 0:
                        pe.wait_ge(xlo_ready, LEAD + G + 1)
                    pe.wait_ge(qk_ready, LEAD + 2 * PAIRS * G + n)
                    cols = slice(pair * 128, (pair + 1) * 128)
                    three(ps[:, QK], w_hi[:, w, cols], w_lo[:, w, cols], xT_hi[par][:], xT_lo[par][:]).then_inc(qk_full, 1)
                elif kind == "value":
                    j = st[2]
                    wait_rot()
                    if j == 0:
                        pe.wait_ge(xlo_ready, LEAD + G + 1)
                    cols = slice(j * S, (j + 1) * S)
                    three(ps[:, ROT], xT_hi[par][:, cols], xT_lo[par][:, cols], w_hi[:, 2], w_lo[:, 2]).then_inc(v_full, 1)
                elif kind == "scores":
                    j, gp = i % GB, (i // GB) % 2
                    if j == 0:
                        pe.wait_ge(qk_ready, LEAD + 2 * PAIRS * (2 * o + i // GB + 1))
                    pe.wait_ge(masked_ready, LEAD + b)
                    cols = slice(j * S, (j + 1) * S)
                    for pair in range(PAIRS):
                        for e in range(2):
                            rows = slice(e * HD, (e + 1) * HD)
                            ins = T.matmul(ps[:, SCORES + e, pair * S:(pair + 1) * S], qT[gp][rows, pair, cols],
                                           kT[gp][rows, pair, cols], start=True, stop=True)
                    ins.then_inc(scores_full, 1)
                elif kind == "probsT":
                    pe.wait_ge(probs_ready, LEAD + b + 1)
                    pe.wait_ge(pTa_ready, LEAD + b)
                    pe.wait_ge(pTb_ready, LEAD + b)
                    for n in range(HEADS):
                        ins = T.transpose(ps[:, PROBST + n // 4, (n % 4) * S:(n % 4 + 1) * S], probs[par][:, n], ident[:])
                        if n == 3:
                            ins.then_inc(pTa_full, 1)
                    ins.then_inc(pTb_full, 1)
                elif kind == "mix":
                    j, gp = i % GB, (i // GB) % 2
                    if j == 0:
                        pe.wait_ge(v_ready, LEAD + GB * (2 * o + i // GB + 1))
                    pe.wait_ge(pTa_ready, LEAD + b + 1)
                    pe.wait_ge(pTb_ready, LEAD + b + 1)
                    pe.wait_ge(mixed_ready, LEAD + b)
                    for n in range(HEADS):
                        head = 2 * (n % PAIRS) + n // PAIRS
                        ins = T.matmul(ps[:, MIX, head * HD:(head + 1) * HD], probsT[:, n], v[gp][:, j, head * HD:(head + 1) * HD],
                                       start=True, stop=True)
                    ins.then_inc(mix_full, 1)
                elif kind == "mixT":
                    pe.wait_ge(mixed_ready, LEAD + b + 1)
                    pe.wait_ge(mixT_ready, LEAD + b)
                    for n in range(PAIRS):
                        ins = T.transpose(ps[:, MIXT, n * S:(n + 1) * S], mixed[:, n * 128:(n + 1) * 128], ident[:])
                    ins.then_inc(mixT_full, 1)
                elif kind == "project":
                    wait_rot()
                    pe.wait_ge(mixT_ready, LEAD + b + 1)
                    for n in range(PAIRS):
                        ins = T.matmul(ps[:, ROT, 0:D], mixedT[:, n], w_o[:, n], start=(n == 0), stop=(n == PAIRS - 1))
                    ins.then_inc(project_full, 1)
                elif kind == "route_normT":
                    wait_rot()
                    pe.wait_ge(normed2_ready, LEAD + G + 1)
                    for j in range(GB):
                        ins = T.transpose(ps[:, ROT, j * S:(j + 1) * S], normed2[par][:, j], ident[:])
                    ins.then_inc(x2T_full, 1)
                elif kind == "route_logits":
                    wait_rot()
                    pe.wait_ge(x2T_ready, LEAD + G + 1)
                    for j in range(GB):
                        ins = T.matmul(ps[:, ROT, j * EXPERTS:(j + 1) * EXPERTS], x2T[:, j * S:(j + 1) * S], w_router[:],
                                       start=True, stop=True)
                    ins.then_inc(logits_full, 1)
                elif kind == "route_ranks":
                    wait_rot()
                    pe.wait_ge(picked_ready, LEAD + G + 1)
                    n = GB * EXPERTS
                    T.matmul(ps[:, ROT, 0:n], earlier[:], picked[:].rearrange("p j e -> p (j e)"), start=True, stop=True)
                    T.matmul(ps[:, ROT, n:2 * n], ones[:], picked[:].rearrange("p j e -> p (j e)"), start=True,
                             stop=True).then_inc(ranks_full, 1)

            def tile(c, q, m, kinds):
                i = 4 * q
                n = c * TILES + i
                if "x" in kinds:
                    k, par = n + m, m % 2
                    pe.wait_ge(xt_in[m], LEAD + 16 * (c * (TILES // 4) + q + 1))
                    pe.wait_ge(x3lo_ready, LEAD + k - 1)
                    T.transpose(ps[:, XB + par, 0:S], xt[m][:], ident[:]).then_inc(x3T_full, 1)
                if "h" in kinds:
                    k, par = n + m - 1, (m - 1) % 2
                    e = pe.value_load(tile_expert[0:1, bass.ds(i + m - 1, 1)], min_val=0, max_val=EXPERTS - 1)
                    pe.wait_ge(act_ready, LEAD + k - 1)
                    cols = bass.ds(e * FC1, FC1)
                    T.matmul(ps[:, HB + par], ones[0:PARTS], b1_parts[:, cols], start=True, stop=False)
                    pe.wait_ge(x3lo_ready, LEAD + k + 1)
                    T.matmul(ps[:, HB + par], x3_hi[par][:], w1_hi[:, cols], start=False, stop=False)
                    T.matmul(ps[:, HB + par], x3_lo[par][:], w1_hi[:, cols], start=False, stop=False)
                    T.matmul(ps[:, HB + par], x3_hi[par][:], w1_lo[:, cols], start=False, stop=True).then_inc(fc1_full, 1)
                if "a" in kinds:
                    k, par = n + m - 2, m % 2
                    pe.wait_ge(act_ready, LEAD + k + 1)
                    pe.wait_ge(actT_ready, LEAD + k - 1)
                    for half in range(2):
                        ins = T.transpose(ps[:, AB + par, half * S:(half + 1) * S], act_out[par][:, half * 128:(half + 1) * 128], ident[:])
                    ins.then_inc(actT_full, 1)
                if "y" in kinds:
                    k, par = n + m - 3, (m - 3) % 2
                    e = pe.value_load(tile_expert[0:1, bass.ds(i + m - 3, 1)], min_val=0, max_val=EXPERTS - 1)
                    pe.wait_ge(y_ready, LEAD + k - 1)
                    T.matmul(ps[:, YB + par, 0:D], ones[0:PARTS], b2_parts[:, bass.ds(e * D, D)], start=True, stop=False)
                    pe.wait_ge(actT_ready, LEAD + k + 1)
                    for half in range(2):
                        ins = T.matmul(ps[:, YB + par, 0:D], actT[par][:, half], w2[:, bass.ds(e * 2 * D + half * D, D)],
                                       start=False, stop=(half == 1))
                    ins.then_inc(fc2_full, 1)

            ROT_STEPS = ("embed", "normT", "value", "project", "route_normT", "route_logits", "route_ranks")
            pe.wait_ge(s_w1, 16 * 5)
            pe.wait_ge(s_bmoved, 16 * 2 * PARTS)

            last_rot = [st for st in octet_steps(True) if st[0] in ROT_STEPS][-1]

            def next_octet(st):
                return (st[0], st[1] - (OB if st[0] == "project" else 2), *st[2:])

            def run(o, steps, before):
                for st in steps:
                    step(o, st, before)
                    if st[0] in ROT_STEPS:
                        before = st

            run(0, first_steps(),
                ("value", -1, 3))
            with pe.Fori(0, chunks) as c:
                run(c * per_chunk, octet_steps(False), ("value", 0, 3))
                if per_chunk > 1:
                    with pe.Fori(1, per_chunk) as i:
                        run(c * per_chunk + i, octet_steps(True), next_octet(last_rot))
                run(c * per_chunk + per_chunk - 1, last_steps(), last_rot)
                pe.wait_ge(ranks_ready, LEAD + 2 * per_chunk * (c + 1))
                pe.wait_ge(table_ready, LEAD + 2 * (c + 1))
                each_tile(pe, c, tile, ("x", "h", "a", "y"), (0, 1, 2, 3))
                pe.wait_ge(y_ready, LEAD + TILES * (c + 1))


def kernel(**i):
    import concourse.bacc as bacc
    from concourse.bass_utils import run_bass_kernel_spmd as run
    nc = bacc.Bacc("TRN2", target_bir_lowering=False, num_devices=1)
    i = {k: np.asarray(v) for k, v in i.items()}
    nseq = i["x"].shape[0]
    nest, seg = i["L0_tok_nest_table"].T, i["L0_tok_seg_table"].T
    laid = {
        "x": i["x"],
        "posT": i["L0_tok_pos_table"][:S].T,
        "w_emb": i["L0_tok_W"],
        "nestT": np.concatenate([nest] * PARTS + [np.zeros((128, PARTS * SEG), nest.dtype)], axis=1),
        "segT": np.concatenate([np.zeros((128, PARTS * NEST), seg.dtype)] + [seg] * PARTS, axis=1),
        "wq": i["L0_attn_wq"].reshape(D, -1), "wk": i["L0_attn_wk"].reshape(D, -1), "wv": i["L0_attn_wv"].reshape(D, -1),
        "bq": i["L0_attn_bq"].reshape(PAIRS, 128).T, "bk": i["L0_attn_bk"].reshape(PAIRS, 128).T,
        "bv": i["L0_attn_bv"].reshape(1, -1), "bo": i["L0_attn_bo"].reshape(1, -1),
        "wo": i["L0_attn_wo"].reshape(-1, D),
        "wr": i["L0_ffn_router_w"].T, "br": i["L0_ffn_router_b"].reshape(1, -1),
        "w1": i["L0_ffn_fc1_w"].transpose(2, 0, 1).reshape(D, -1),
        "w2": i["L0_ffn_fc2_w"].reshape(EXPERTS, D, 2, 128).transpose(3, 0, 2, 1).reshape(128, -1),
        "b1": i["L0_ffn_fc1_b"], "b2": i["L0_ffn_fc2_b"],
    }
    laid = {k: np.ascontiguousarray(v) for k, v in laid.items()}
    a = {k: nc.dram_tensor("in_" + k, v.shape, mybir.dt.from_np(v.dtype), kind="ExternalInput").ap() for k, v in laid.items()}
    out = nc.dram_tensor("out_h", (nseq, S, D), mybir.dt.float32, kind="ExternalOutput").ap()
    hmid = nc.dram_tensor("hmid", (nseq, S, D), mybir.dt.float32, kind="Internal").ap()
    rows = EXPERTS * ((nseq // (4 if nseq == 128 else 2)) * S + S) + EXPERTS * S
    xs = nc.dram_tensor("xs", (rows, D), mybir.dt.float32, kind="Internal").ap()
    spare = nc.dram_tensor("spare", (3, D), mybir.dt.float32, kind="Internal").ap()
    ys = nc.dram_tensor("ys", (rows, D), mybir.dt.float32, kind="Internal").ap()
    codes = nc.dram_tensor("codes", (2, (nseq + OB) * S), mybir.dt.bfloat16, kind="Internal").ap()
    build(nc, a, out, hmid, codes, xs, ys, spare, nseq)
    r = run(nc, [{"in_" + k: v for k, v in laid.items()}], core_ids=[0])
    return r.results[0]["out_h"]
```

```python
import numpy as np
import concourse.bass as bass
from concourse import mybir
from concourse.alu_op_type import AluOpType as ALU
from contextlib import ExitStack

S = 128
D = 128
HEADS, HD = 8, 64
PAIRS = HEADS // 2
NEST, SEG = 16, 8
PARTS = 3
CODES = PARTS * (NEST + SEG)
EXPERTS, HID = 8, 256
FC1 = 2 * HID
GB = 4
OB = 2 * GB
NEG_INF = -10000000000.0
HUGE = 3.0e38
EPS = 1e-5
TABLE_STEPS = 17
LEAD = 64
SW_LEAD = 16


def octet_steps(previous, combine):
    steps = []

    def combining(*step):
        if combine:
            steps.append(step)

    def late(*step):
        if step[1] >= 0 or previous:
            steps.append(step)

    for k in range(OB):
        half, n = k // GB, k % GB
        g = half - 1
        steps.append(("scores", k))
        if k == 0:
            combining("total_load", 0)
            combining("total_load", 1)
            combining("total_rows", 0)
        if k == 5:
            combining("total_store", 0)
        combining("gather", k)
        steps.append(("query", half + 1, n))
        late("probsT", k - 1)
        steps.append(("max", k))
        steps.append(("value", half + 1, n))
        steps.append(("key", half + 1, n))
        late("mix", k - 1)
        steps.append(("exp", k, 0))
        late("project", k - 2)
        if n == 0:
            late("route_choose", g - 1)
        elif n == 1:
            late("route_rows", g - 1)
        elif n == 2:
            late("route_scale", g)
        elif n == 3:
            late("route_logits", g)
        late("mixT", k - 1)
        if n == 0:
            steps.append(("onehot", half + 2))
            late("route_ranks", g - 1)
        elif n == 1:
            steps.append(("embed", half + 2))
            late("route_norm", g)
            late("scatter", g - 1, 0)
        elif n == 2:
            late("route_normT", g)
            steps.append(("norm", half + 2))
            late("scatter", g - 1, 1)
            late("route_weight", g - 1)
        elif n == 3:
            steps.append(("normT", half + 2))
            steps.append(("residual", half + 1))
        steps.append(("exp", k, 1))
        for j in {0: [k - 1], 3: [k - 3, k - 2, k - 1]}.get(n, []):
            if j >= 0:
                combining("total", j)
    combining("total", OB - 1)
    combining("total_store", 1)
    return steps


def combine_steps():
    return [st for st in octet_steps(False, True) if st not in octet_steps(False, False)]


def last_steps():
    return [(st[0], st[1] + (OB if st[0] in ("project", "probsT", "mix", "mixT") else 2), *st[2:])
            for st in octet_steps(True, False) if st[1] < 0]


def first_steps():
    return ([(w, g) for g in range(2) for w in ("onehot", "embed", "norm", "normT")] + [("residual", 0)] +
            [(w, 0, n) for n in range(PAIRS) for w in ("query", "value", "key")])


def build(nc, a, out, hmid, codes_dram, xs, ys, spare, nseq):
    F32, F32R, BF16, I32 = mybir.dt.float32, mybir.dt.float32r, mybir.dt.bfloat16, mybir.dt.int32
    ACT = mybir.ActivationFunctionType
    AX = mybir.AxisListType.X
    groups = nseq // GB
    octets = nseq // OB
    chunks = 4 if nseq == 128 else 2
    per_chunk = octets // chunks
    U32 = mybir.dt.uint32
    R = per_chunk * OB * S + S
    TILES = 2 * per_chunk * OB + EXPERTS
    BLOCKS = (EXPERTS * R + EXPERTS * S) // S
    QUADS = TILES // 4
    ctx = ExitStack()
    with ctx:
        def sb(name, shape, dt=F32):
            return ctx.enter_context(nc.sbuf_tensor(name, shape, dt))

        def sem(name):
            return ctx.enter_context(nc.semaphore(name))

        led = []

        def led_sem(name):
            s = sem(name)
            led.append(s)
            return s

        ident = sb("ident", [128, 128])
        causal = sb("causal", [128, 128])
        part_code = sb("part_code", [CODES, 1])
        part_mask = sb("part_mask", [CODES, PARTS])
        small = sb("small", [CODES, 4])
        posT = sb("posT", [128, S]); nestT = sb("nestT", [128, CODES]); segT = sb("segT", [128, CODES])
        w_emb = sb("w_emb", [128, 3, D])
        pos_emb = sb("pos_emb", [S, D])
        code_table = sb("code_table", [CODES, D], BF16)
        w_hi = sb("w_hi", [128, 3, HEADS * HD], F32R)
        w_lo = sb("w_lo", [128, 3, HEADS * HD], F32R)
        bias_qk = sb("bias_qk", [128, 2, PAIRS])
        bias_q8 = sb("bias_q8", [128, PAIRS])
        bias_vT = sb("bias_vT", [128, PAIRS])
        bias_v = sb("bias_v", [128, PAIRS, S])
        bias_o = sb("bias_o", [128, D])
        w_o = sb("w_o", [128, PAIRS, D])

        code_rows = [sb(f"code_rows{i}", [CODES, GB * S], BF16) for i in range(2)]
        onehot = sb("onehot", [CODES, GB * S], BF16)
        h = [sb(f"h{i}", [S, GB, D]) for i in range(2)]
        stats = sb("stats", [S, GB, 6]); moments = sb("moments", [S, GB, 2])
        var_eps = sb("var_eps", [S, GB]); rstd = sb("rstd", [S, GB]); minus_half = sb("minus_half", [S, GB])
        normed = sb("normed", [S, GB, D])
        xT_hi = [sb(f"xT_hi{i}", [D, GB * S], F32R) for i in range(2)]
        xT_lo = [sb(f"xT_lo{i}", [D, GB * S], F32R) for i in range(2)]
        qT = [sb(f"qT{i}", [128, PAIRS, GB * S]) for i in range(2)]
        kT = [sb(f"kT{i}", [128, PAIRS, GB * S]) for i in range(2)]
        v = [sb(f"v{i}", [S, GB, HEADS * HD]) for i in range(2)]

        taken = [0, 0]

        def scratch(room, parts, cols, dt=F32):
            at = taken[room]
            n = cols // 2 if dt == BF16 else cols
            taken[room] += n
            t = v[room][0:parts].rearrange("p a b -> p (a b)")[:, at:at + n]
            return t if dt == F32 else t.bitcast(dt)

        x_raw = scratch(0, nseq, S, I32)
        scan = [scratch(0, nseq, S) for _ in range(4)]
        seg_int = scratch(0, nseq, S, I32)
        codes_sb = scratch(0, nseq, 2 * S, BF16).rearrange("p (a s) -> p a s", a=2)
        t_full, t_rest, t_rest2, t_acc = [scratch(0, CODES, D) for _ in range(4)]
        t_hi, t_mid, t_lo = [scratch(0, CODES, D, BF16) for _ in range(3)]
        b12, b_rest = [sb(f"b12_{i}", [PARTS * EXPERTS, FC1 + D]) for i in range(2)]
        b_hi, b_mid, b_parts = [sb(f"b_part{i}", [PARTS * EXPERTS, FC1 + D], BF16) for i in range(3)]
        w_raw = qT[0][:, 0:3]

        masked = [sb(f"masked{i}", [S, HEADS, S]) for i in range(2)]
        neg_max = [sb(f"neg_max{i}", [S, HEADS]) for i in range(2)]
        probs = [sb(f"probs{i}", [S, HEADS, S]) for i in range(2)]
        sums = [sb(f"sums{i}", [S, HEADS]) for i in range(2)]
        inv_sums = sb("inv_sums", [S, HEADS])
        probsT = sb("probsT", [S, HEADS, S])
        mixed = sb("mixed", [S, HEADS * HD])
        mixedT = sb("mixedT", [128, PAIRS, S])
        h2 = [sb(f"h2_{i}", [S, GB, D]) for i in range(2)]
        residual = [sb(f"residual{i}", [S, GB, D]) for i in range(2)]

        earlier = sb("earlier", [128, 128], BF16)
        ones = sb("ones", [128, 128], BF16)
        expert_no = sb("expert_no", [S, EXPERTS])
        region = sb("region", [S, EXPERTS])
        w_router = sb("w_router", [D, EXPERTS]); bias_r = sb("bias_r", [S, EXPERTS])
        moments2 = sb("moments2", [S, GB, 2]); stats2 = sb("stats2", [S, GB, 6])
        var_eps2 = sb("var_eps2", [S, GB]); rstd2 = sb("rstd2", [S, GB])
        normed2 = [sb(f"normed2_{i}", [S, GB, D]) for i in range(2)]
        x2T = sb("x2T", [D, GB * S])
        logits = sb("logits", [S, GB, EXPERTS]); top = sb("top", [S, GB, EXPERTS]); top_at = sb("top_at", [S, GB, EXPERTS], U32)
        top_no = sb("top_no", [S, GB, 2]); chosen = sb("chosen", [S, 2, GB, EXPERTS]); picked = sb("picked", [S, GB, EXPERTS], BF16)
        gap = sb("gap", [S, GB]); gap_exp = sb("gap_exp", [S, GB]); gap_one = sb("gap_one", [S, GB])
        ranks = sb("ranks", [S, 2, GB, EXPERTS]); filled = sb("filled", [S, GB + 1, EXPERTS])
        rows_f = sb("rows_f", [S, GB, EXPERTS]); rows_2 = sb("rows_2", [S, 2, GB, EXPERTS]); row_f = sb("row_f", [S, 2, GB])
        row = [sb(f"row{i}", [S, 2, GB], I32) for i in range(2)]
        weight = sb("weight", [S, 2, GB])
        rows_all = sb("rows_all", [S, 2, per_chunk * OB], I32)
        weights_all = sb("weights_all", [S, 2, per_chunk * OB])
        ends = sb("ends", [1, EXPERTS], I32)
        tile_no = sb("tile_no", [1, TILES]); tiles_f = sb("tiles_f", [1, EXPERTS]); tiles_i = sb("tiles_i", [1, EXPERTS], I32)
        tiles_end = sb("tiles_end", [1, EXPERTS]); passed = masked[0][0:1].rearrange("p a b -> p (a b)")[:, 0:TILES * EXPERTS].rearrange("p (t e) -> p t e", e=EXPERTS)
        tab = sb("tab", [1, 4, TILES]); blocks_f = sb("blocks_f", [1, TILES // 2]); tile_blocks = sb("tile_blocks", [1, TILES // 2], I32); experts_f = sb("experts_f", [1, TILES]); packed = sb("packed", [1, QUADS]); quad_experts = sb("quad_experts", [1, QUADS], I32)
        zeros = sb("zeros", [S, D])

        w1_hi = sb("w1_hi", [D, EXPERTS * FC1], F32R); w1_lo = sb("w1_lo", [D, EXPERTS * FC1], F32R)
        w1_raw = [kT[1], qT[1]]
        w2 = sb("w2", [128, EXPERTS * 2 * D])
        b_mask = sb("b_mask", [PARTS * EXPERTS, PARTS])
        b1_parts = sb("b1_parts", [PARTS, EXPERTS * FC1], BF16); b2_parts = sb("b2_parts", [PARTS, EXPERTS * D], BF16)
        table_in = sb("table_in", [S, 1])
        gate = [sb(f"gate{i}", [S, HID]) for i in range(2)]
        xt = [probs[0][:, i * GB:(i + 1) * GB] for i in range(2)]
        y = [probs[1][:, i * GB:(i + 1) * GB] for i in range(2)]
        x3_hi = [xT_hi[0], sb("x3_hi", [D, GB * S], F32R)]; x3_lo = [xT_lo[0], sb("x3_lo", [D, GB * S], F32R)]
        act_out = [masked[1][:, 2 * i:2 * i + 2].rearrange("p a s -> p (a s)") for i in range(4)]
        actT = [probsT[:, 2 * i:2 * i + 2] for i in range(4)]

        rows_now = sb("rows_now", [S, 2, OB], I32); weights_now = sb("weights_now", [S, 2, OB])
        y_rows = [sb(f"y_rows{i}", [S, 2, D]) for i in range(4)]
        total = [sb(f"total{i}", [S, GB, D]) for i in range(2)]

        ps = ctx.enter_context(nc.psum_tensor("ps", [128, 8, 512], F32))
        SCORES, PROBST, MIX, MIXT, QK, ROT = 0, 2, 4, 5, 6, 7

        s_const = sem("s_const"); s_x = sem("s_x"); s_w = sem("s_w"); s_wqkv = sem("s_wqkv"); s_codes = sem("s_codes")
        s_codes_out = sem("s_codes_out"); s_pool = sem("s_pool"); s_dve = sem("s_dve"); s_table_ps = sem("s_table_ps")
        s_table = sem("s_table"); s_whi = sem("s_whi"); s_wlo = sem("s_wlo"); s_bias_v = sem("s_bias_v"); s_bias_o_ps = sem("s_bias_o_ps"); s_bias_o = sem("s_bias_o")
        codes_in = [led_sem("codes_in0"), led_sem("codes_in1")]
        onehot_ready = led_sem("onehot_ready"); embed_full = led_sem("embed_full"); embedded = led_sem("embedded")
        moments_ready = led_sem("moments_ready"); normed_ready = led_sem("normed_ready"); normT_full = led_sem("normT_full")
        xhi_ready = led_sem("xhi_ready"); xlo_ready = led_sem("xlo_ready")
        qk_full = led_sem("qk_full"); qk_ready = led_sem("qk_ready"); v_full = led_sem("v_full"); v_ready = led_sem("v_ready")
        scores_full = led_sem("scores_full"); masked_ready = led_sem("masked_ready"); max_ready = led_sem("max_ready")
        probs_ready = led_sem("probs_ready"); pTa_full = led_sem("pTa_full"); pTb_full = led_sem("pTb_full")
        pTa_ready = led_sem("pTa_ready"); pTb_ready = led_sem("pTb_ready"); mix_full = led_sem("mix_full")
        mixed_ready = led_sem("mixed_ready"); mixT_full = led_sem("mixT_full"); mixT_ready = led_sem("mixT_ready")
        project_full = led_sem("project_full"); h2_ready = led_sem("h2_ready")
        h2_stored = [led_sem("h2_stored0"), led_sem("h2_stored1")]
        var_ready = led_sem("var_ready"); var2_ready = led_sem("var2_ready"); rstd_ready = led_sem("rstd_ready"); rstd2_ready = led_sem("rstd2_ready")
        bn_done = led_sem("bn_done"); inv_ready = led_sem("inv_ready");
        p_own = sem("p_own")
        residual_ready = led_sem("residual_ready")
        bn2_done = led_sem("bn2_done"); moments2_ready = led_sem("moments2_ready"); normed2_ready = led_sem("normed2_ready")
        x2T_full = led_sem("x2T_full"); x2T_ready = led_sem("x2T_ready"); logits_full = led_sem("logits_full")
        logits_ready = led_sem("logits_ready"); top_ready = led_sem("top_ready"); top_at_ready = led_sem("top_at_ready")
        top_no_ready = led_sem("top_no_ready"); gap_ready = led_sem("gap_ready"); chosen_ready = led_sem("chosen_ready")
        picked_ready = led_sem("picked_ready"); gap_exp_ready = led_sem("gap_exp_ready")
        gap_one_ready = led_sem("gap_one_ready"); weight0_ready = led_sem("weight0_ready"); weight1_ready = led_sem("weight1_ready")
        weights_kept = led_sem("weights_kept"); ranks_full = led_sem("ranks_full"); ranks_ready = led_sem("ranks_ready")
        filled_step = led_sem("filled_step"); rows_a = led_sem("rows_a"); rows_b = led_sem("rows_b"); rows_c = led_sem("rows_c")
        row_ready = led_sem("row_ready"); rows_kept = led_sem("rows_kept"); filled_next = led_sem("filled_next")
        scattered = [sem("scattered0"), sem("scattered1")]
        filled_start = led_sem("filled_start"); ends_ready = led_sem("ends_ready"); padded = led_sem("padded")
        table_own = led_sem("table_own"); table_ready = led_sem("table_ready")
        xt_in = [led_sem(f"xt_in{i}") for i in range(2)]
        x3T_full = led_sem("x3T_full"); x3hi_ready = led_sem("x3hi_ready"); x3lo_ready = led_sem("x3lo_ready")
        fc1_full = led_sem("fc1_full"); gate_ready = led_sem("gate_ready"); act_ready = led_sem("act_ready")
        actT_full = led_sem("actT_full"); actT_ready = led_sem("actT_ready"); fc2_full = led_sem("fc2_full")
        y_ready = led_sem("y_ready"); y_stored = [led_sem(f"y_stored{i}") for i in range(2)]
        rows_now_ready = led_sem("rows_now_ready"); weights_now_ready = led_sem("weights_now_ready")
        y_in = [sem(f"y_in{i}") for i in range(4)]
        silu_in = led_sem("silu_in"); h_in = [led_sem("h_in0"), led_sem("h_in1")]; half_total = led_sem("half_total"); total_ready = led_sem("total_ready")
        out_stored = [led_sem("out_stored0"), led_sem("out_stored1")]
        s_w1 = sem("s_w1"); s_w1hi = sem("s_w1hi"); s_w1lo = sem("s_w1lo"); s_bias = sem("s_bias"); s_bparts = sem("s_bparts")
        s_bmoved = sem("s_bmoved"); s_zero = sem("s_zero"); s_yzero = sem("s_yzero"); wait_carried = sem("wait_carried"); s_trash = sem("s_trash")

        block = ctx.enter_context(nc.Block())
        hview = hmid.rearrange("(g j) s d -> g s j d", j=GB)

        def carry_wait(eng):
            eng.sem_inc(wait_carried, 1)

        XB, HB, AB, YB = 0, 1, 5, 7

        def each_quad(eng, c, quad):
            with eng.Fori(0, QUADS // 2 - 1) as pair:
                quad(c, pair, 0)
                quad(c, pair, 1)
            quad(c, QUADS // 2 - 1, 0)
            quad(c, QUADS // 2 - 1, 1, last=True)

        def each_chunk(eng, chunk):
            chunk(0, False)
            with eng.Fori(1, chunks) as c:
                chunk(c, True)

        @block.sync
        def _(sp):
            for s in led:
                sp.sem_inc(s, LEAD)
            sp.dma_start(x_raw[:], a["x"]).then_inc(s_x, 16)
            sp.dma_start(posT[:], a["posT"]).then_inc(s_w, 16)
            sp.dma_start(w_emb[:], a["w_emb"].rearrange("(c p) n -> p c n", c=3)).then_inc(s_w, 16)
            sp.dma_start(nestT[:], a["nestT"]).then_inc(s_w, 16)
            sp.dma_start(segT[:], a["segT"]).then_inc(s_w, 16)
            for n, w in enumerate(("wq", "wk", "wv")):
                sp.dma_start(w_raw[:, n], a[w]).then_inc(s_wqkv, 16)
            sp.dma_start(bias_qk[:, 0], a["bq"]).then_inc(s_wqkv, 16)
            sp.dma_start(bias_qk[:, 1], a["bk"]).then_inc(s_wqkv, 16)
            sp.dma_start(bias_vT[:], a["bv"]).then_inc(s_wqkv, 16)
            sp.dma_start(bias_o[:], a["bo"].broadcast_to([128, D])).then_inc(s_wqkv, 16)
            sp.dma_start(w_o[:], a["wo"].rearrange("(c p) n -> p c n", c=PAIRS)).then_inc(s_wqkv, 16)
            sp.dma_start(w1_raw[0][:].rearrange("p a b -> p (a b)"), a["w1"][:, 0:EXPERTS * FC1 // 2]).then_inc(s_w1, 16)
            sp.dma_start(w1_raw[1][:].rearrange("p a b -> p (a b)"), a["w1"][:, EXPERTS * FC1 // 2:]).then_inc(s_w1, 16)
            sp.dma_start(w2[:], a["w2"]).then_inc(s_w1, 16)
            sp.dma_start(w_router[:], a["wr"]).then_inc(s_w1, 16)
            sp.dma_start(bias_r[:], a["br"].broadcast_to([S, EXPERTS])).then_inc(s_w1, 16)
            for n in range(PARTS):
                sp.dma_start(b12[n * EXPERTS:(n + 1) * EXPERTS, 0:FC1], a["b1"]).then_inc(s_bias, 16)
                sp.dma_start(b12[n * EXPERTS:(n + 1) * EXPERTS, FC1:], a["b2"]).then_inc(s_bias, 16)
            sp.wait_ge(s_codes, 2)
            cd = codes_dram.rearrange("k (b s) -> b k s", s=S)
            sp.dma_start(cd[0:nseq], codes_sb[:]).then_inc(s_codes_out, 16)
            sp.dma_start(cd[nseq:nseq + OB], codes_sb[0:OB]).then_inc(s_codes_out, 16)
            sp.wait_ge(s_codes_out, 32)

            def load_codes(G, par):
                sp.wait_ge(onehot_ready, LEAD + G - 1)
                sp.dma_start(code_rows[par][0:PARTS * NEST], codes_dram[0:1, bass.ds(G * GB * S, GB * S)].broadcast_to([PARTS * NEST, GB * S])).then_inc(codes_in[par], 16)
                sp.dma_start(code_rows[par][PARTS * NEST:CODES], codes_dram[1:2, bass.ds(G * GB * S, GB * S)].broadcast_to([PARTS * SEG, GB * S])).then_inc(codes_in[par], 16)

            def fill(n):
                if n == 0:
                    sp.dma_start(ys[EXPERTS * R:].rearrange("(p r) d -> p r d", p=S),
                                 zeros[:].unsqueeze(1).broadcast_to([S, EXPERTS, D])).then_inc(s_yzero, 16)
                sp.dma_start(ys[n * R:(n + 1) * R].rearrange("(p r) d -> p r d", p=S),
                             zeros[:].unsqueeze(1).broadcast_to([S, R // S, D])).then_inc(s_yzero, 16)

            def octet(o, c, steps, before=True):
                for st in steps:
                    if st[0] == "scores" and not before:
                        fill(st[1])
                    if st[0] in ("total_load", "total_store"):
                        combine(o - per_chunk, c - 1, st)
                    if st == ("scores", 0):
                        load_codes(2 * o + 2, 0)
                    if st == ("scores", 4):
                        load_codes(2 * o + 3, 1)
                    if st[0] == "route_norm":
                        G = 2 * o + st[1]
                        sp.wait_ge(h2_ready, LEAD + GB * (G + 1))
                        sp.dma_start(hview[G], h2[st[1] % 2][:]).then_inc(h2_stored[st[1] % 2], 16)

            def pad(c):
                sp.wait_ge(ends_ready, LEAD + c + 1)
                carry_wait(sp)
                for e in range(EXPERTS):
                    end = sp.value_load(ends[0:1, e:e + 1], min_val=0, max_val=EXPERTS * R - S)
                    sp.dma_start(xs[bass.ds(end, S)], zeros[:]).then_inc(padded, 16)
                sp.wait_ge(padded, LEAD + 16 * EXPERTS * (c + 1))
                for par in range(2):
                    sp.wait_ge(scattered[par], SW_LEAD + 16 * 2 * GB * per_chunk * (c + 1))
                sp.wait_ge(s_yzero, 16 * (EXPERTS + 1))
                for slot in range(4):
                    sp.wait_ge(y_in[slot], SW_LEAD + 64 * per_chunk * c)
                sp.wait_ge(table_ready, LEAD + 2 * (c + 1))

            def rows_of(pair, z, half):
                blocks = sp.value_load(tile_blocks[0:1, bass.ds(4 * pair + 2 * z + half, 1)], min_val=0, max_val=(BLOCKS - 1) * 513)
                return [nc.s_assert_within(b * S, 0, (BLOCKS - 1) * S) for b in (blocks & 511, blocks >> 9)]

            def load_quad(c, pair, z):
                sp.wait_ge(x3T_full, LEAD + c * QUADS + 2 * pair + z - 1)
                carry_wait(sp)
                for half in range(2):
                    for j, first in enumerate(rows_of(pair, z, half)):
                        sp.dma_start(xt[z][:, 2 * half + j], xs[bass.ds(first, S)]).then_inc(xt_in[z], 16)

            def quad(c, pair, z, load=True):
                if load:
                    load_quad(c, pair + 1 + z, 1 - z)
                sp.wait_ge(y_ready, LEAD + c * QUADS + 2 * pair + z + 1)
                carry_wait(sp)
                for half in range(2):
                    for j, first in enumerate(rows_of(pair, z, half)):
                        sp.dma_start(ys[bass.ds(first, S)], y[z][:, 2 * half + j]).then_inc(y_stored[z], 16)

            def combine(o, c, st):
                half = st[1]
                if st[0] == "total_load":
                    sp.wait_ge(out_stored[half], LEAD + 16 * o)
                    for par in range(2):
                        sp.wait_ge(h2_stored[par], LEAD + 16 * per_chunk * (c + 1))
                    sp.dma_start(total[half][:], hmid.rearrange("(o h j) s d -> o h s j d", h=2, j=GB)[o, half]).then_inc(h_in[half], 16)
                else:
                    sp.wait_ge(total_ready, LEAD + OB * o + GB * (half + 1))
                    sp.dma_start(out.rearrange("(o h j) s d -> o h s j d", h=2, j=GB)[o, half], total[half][:]).then_inc(out_stored[half], 16)

            load_codes(0, 0)
            load_codes(1, 1)
            sp.wait_ge(s_zero, 1)
            for n in range(EXPERTS):
                sp.dma_start(xs[EXPERTS * R + n * S:EXPERTS * R + (n + 1) * S], zeros[:]).then_inc(s_trash, 16)
            sp.wait_ge(s_trash, 16 * EXPERTS)
            sp.wait_ge(s_bparts, 1)
            for n in range(PARTS):
                sp.dma_start(b1_parts[n:n + 1].rearrange("p (e n) -> p e n", e=EXPERTS), b_parts[n * EXPERTS:(n + 1) * EXPERTS, 0:FC1]).then_inc(s_bmoved, 16)
                sp.dma_start(b2_parts[n:n + 1].rearrange("p (e n) -> p e n", e=EXPERTS), b_parts[n * EXPERTS:(n + 1) * EXPERTS, FC1:]).then_inc(s_bmoved, 16)

            def chunk(c, before):
                octet(c * per_chunk, c, octet_steps(False, before), before)
                if per_chunk > 1:
                    with sp.Fori(1, per_chunk) as i:
                        octet(c * per_chunk + i, c, octet_steps(True, before))
                octet(c * per_chunk + per_chunk - 1, c, last_steps())
                pad(c)
                load_quad(c, 0, 0)
                load_quad(c, 0, 1)
                load_quad(c, 1, 0)
                with sp.Fori(0, QUADS // 2 - 2) as pair:
                    quad(c, pair, 0)
                    quad(c, pair, 1)
                quad(c, QUADS // 2 - 2, 0)
                quad(c, QUADS // 2 - 2, 1, load=False)
                for z in range(2):
                    quad(c, QUADS // 2 - 1, z, load=False)

            each_chunk(sp, chunk)
            with sp.Fori(0, per_chunk) as i:
                for st in combine_steps():
                    if st[0] in ("total_load", "total_store"):
                        combine((chunks - 1) * per_chunk + i, chunks - 1, st)
            for half in range(2):
                sp.wait_ge(out_stored[half], LEAD + 16 * octets)

        @block.gpsimd
        def _(pool):
            own = [0]

            def link(ins):
                own[0] += 1
                ins.then_inc(p_own, 1)
                pool.wait_ge(p_own, own[0])

            link(pool.memset(ident[:], 0.0))
            link(pool.affine_select(out=ident[:], in_=ident[:], compare_op=ALU.not_equal, fill=1.0, base=0,
                                    pattern=[[-1, 128]], channel_multiplier=1))
            link(pool.memset(causal[:], HUGE))
            link(pool.affine_select(out=causal[:], in_=causal[:], compare_op=ALU.is_ge, fill=NEG_INF, base=0,
                                    pattern=[[-1, 128]], channel_multiplier=1))
            link(pool.memset(ones[:], 1.0))
            link(pool.memset(earlier[:], 1.0))
            link(pool.affine_select(out=earlier[:], in_=earlier[:], compare_op=ALU.is_gt, fill=0.0, base=0,
                                    pattern=[[1, 128]], channel_multiplier=-1))
            link(pool.iota(expert_no[:], pattern=[[1, EXPERTS]], base=0, channel_multiplier=0,
                      allow_small_or_imprecise_dtypes=True))
            link(pool.iota(region[:], pattern=[[R, EXPERTS]], base=0, channel_multiplier=0,
                      allow_small_or_imprecise_dtypes=True))
            link(pool.iota(tile_no[:], pattern=[[1, TILES]], base=0, channel_multiplier=0,
                      allow_small_or_imprecise_dtypes=True))
            pool.memset(zeros[:], 0.0).then_inc(s_zero, 1)
            pool.memset(minus_half[:], -0.5).then_inc(s_pool, 1)
            pool.iota(small[:, 0:1], pattern=[[0, 1]], base=0, channel_multiplier=1,
                      allow_small_or_imprecise_dtypes=True).then_inc(s_const, 1)

            def step(o, st):
                kind, i = st[0], st[1]
                if kind == "embed":
                    G = 2 * o + i
                    pool.wait_ge(moments_ready, LEAD + G + 1)
                    pool.wait_ge(normed_ready, LEAD + G)
                    carry_wait(pool)
                    pool.tensor_scalar(var_eps[:], moments[:, :, 1], EPS, None, ALU.add).then_inc(var_ready, 1)
                    pool.wait_ge(var_ready, LEAD + G + 1)
                    pool.tensor_tensor(rstd[:], var_eps[:], minus_half[:], ALU.pow).then_inc(rstd_ready, 1)
                elif kind == "route_norm":
                    G = 2 * o + i
                    pool.wait_ge(moments2_ready, LEAD + G + 1)
                    pool.wait_ge(normed2_ready, LEAD + G)
                    carry_wait(pool)
                    pool.tensor_scalar(var_eps2[:], moments2[:, :, 1], EPS, None, ALU.add).then_inc(var2_ready, 1)
                    pool.wait_ge(var2_ready, LEAD + G + 1)
                    pool.tensor_tensor(rstd2[:], var_eps2[:], minus_half[:], ALU.pow).then_inc(rstd2_ready, 1)
                elif kind == "residual":
                    G = 2 * o + i
                    pool.wait_ge(embedded, LEAD + G + 1)
                    pool.wait_ge(h2_ready, LEAD + GB * (G - 1))
                    pool.tensor_tensor(residual[i % 2][:], h[i % 2][:], bias_o[:].unsqueeze(1).broadcast_to([S, GB, D]),
                                       ALU.add).then_inc(residual_ready, 1)
                elif kind == "route_choose":
                    G = 2 * o + i
                    pool.wait_ge(chosen_ready, LEAD + 2 * (G + 1))
                    pool.wait_ge(ranks_full, LEAD + G)
                    pool.tensor_tensor(picked[:], chosen[:, 0], chosen[:, 1], ALU.add).then_inc(picked_ready, 1)
                elif kind == "route_ranks":
                    G = 2 * o + i
                    pool.wait_ge(ranks_ready, LEAD + G + 1)
                    for j in range(GB):
                        pool.tensor_tensor(filled[:, j + 1], filled[:, j], ranks[:, 1, j], ALU.add).then_inc(filled_step, 1)
                        pool.wait_ge(filled_step, LEAD + GB * G + j + 1)
                    pool.tensor_tensor(rows_f[:], ranks[:, 0], filled[:, 0:GB], ALU.add).then_inc(rows_c, 1)
                    pool.wait_ge(rows_c, LEAD + G + 1)
                    for k in range(2):
                        pool.tensor_tensor(rows_2[:, k], rows_f[:], chosen[:, k], ALU.mult).then_inc(rows_a, 1)
                    pool.tensor_copy(filled[:, 0], filled[:, GB]).then_inc(filled_next, 1)
                elif kind == "route_rows":
                    G, par = 2 * o + i, i % 2
                    pool.wait_ge(row_ready, LEAD + G + 1)
                    carry_wait(pool)
                    pool.tensor_copy(rows_all[:, :, bass.ds(place(o, i), GB)], row[par][:]).then_inc(rows_kept, 1)
                elif kind == "scatter":
                    par, k = i % 2, st[2]
                    for j in range(GB):
                        pool.indirect_dma_start(xs, bass.IndirectOffsetOnAxis(ap=row[par][:, k, j:j + 1].bitcast(U32), axis=0),
                                                normed2[par][:, j], None).then_inc(scattered[par], 16)
                elif kind == "route_weight":
                    G = 2 * o + i
                    pool.wait_ge(weight1_ready, LEAD + G + 1)
                    carry_wait(pool)
                    pool.tensor_copy(weights_all[:, :, bass.ds(place(o, i), GB)], weight[:]).then_inc(weights_kept, 1)

            def place(o, i):
                return (2 * local[0] + i) * GB

            local = [0]

            def combine(o, c, i, st):
                if st[0] == "total_rows":
                    for z in range(2):
                        pool.wait_ge(y_stored[z], LEAD + 64 * (QUADS // 2) * (c + 1))
                    for slot in range(4):
                        pool.wait_ge(y_in[slot], SW_LEAD + 64 * o)
                    carry_wait(pool)
                    pool.tensor_copy(rows_now[:], rows_all[:, :, bass.ds(i * OB, OB)]).then_inc(rows_now_ready, 1)
                    pool.wait_ge(total_ready, LEAD + OB * o)
                    pool.wait_ge(rows_now_ready, LEAD + o + 1)
                    carry_wait(pool)
                    pool.tensor_copy(weights_now[:], weights_all[:, :, bass.ds(i * OB, OB)]).then_inc(weights_now_ready, 1)
                    pool.wait_ge(weights_now_ready, LEAD + o + 1)
                elif st[0] == "gather":
                    j = st[1]
                    pool.wait_ge(total_ready, LEAD + OB * o + j - 3)
                    carry_wait(pool)
                    for k in range(2):
                        pool.indirect_dma_start(y_rows[j % 4][:, k], None, ys,
                                                bass.IndirectOffsetOnAxis(ap=rows_now[:, k, j:j + 1].bitcast(U32), axis=0)).then_inc(y_in[j % 4], 16)

            pool.wait_ge(s_zero, 1)
            for n, s in enumerate(scattered + y_in):
                pool.dma_start(spare[n:n + 1], zeros[0:1]).then_inc(s, SW_LEAD)
            pool.wait_ge(s_bias_o, 1)
            pool.wait_ge(s_pool, 1)
            for st in first_steps():
                step(0, st)

            def octet(c, i, steps):
                local[0] = i
                for st in steps:
                    step(c * per_chunk + i, st)
                    combine((c - 1) * per_chunk + i, c - 1, i, st)

            def chunk(c, before):
                pool.wait_ge(table_ready, LEAD + 2 * c)
                pool.wait_ge(filled_next, LEAD + 2 * per_chunk * c)
                pool.wait_ge(ends_ready, LEAD + c)
                carry_wait(pool)
                pool.tensor_copy(filled[:, 0], region[:]).then_inc(filled_start, 1)
                pool.wait_ge(filled_start, LEAD + c + 1)
                octet(c, 0, octet_steps(False, before))
                if per_chunk > 1:
                    with pool.Fori(1, per_chunk) as i:
                        octet(c, i, octet_steps(True, before))
                steps = last_steps()
                n = steps.index(("route_ranks", 1)) + 1
                octet(c, per_chunk - 1, steps[:n])
                pool.wait_ge(filled_next, LEAD + 2 * per_chunk * (c + 1))
                carry_wait(pool)
                pool.tensor_copy(ends[:], filled[0:1, 0]).then_inc(ends_ready, 1)
                octet(c, per_chunk - 1, steps[n:])

            each_chunk(pool, chunk)
            with pool.Fori(0, per_chunk) as i:
                for st in combine_steps():
                    combine((chunks - 1) * per_chunk + i, chunks - 1, i, st)

        @block.scalar
        def _(act):
            act.wait_ge(s_zero, 1)
            act.wait_ge(s_wqkv, 16 * 8)
            nc.scalar.mul(bias_q8[:], bias_qk[:, 0], HD ** -0.5).then_inc(s_whi, 1)
            nc.scalar.copy(w_hi[:], w_raw[:]).then_inc(s_whi, 1)
            chunk_now = [0]

            def halve(c, pair, z):
                act.wait_ge(x3T_full, LEAD + c * QUADS + 2 * pair + z + 1)
                nc.scalar.copy(x3_hi[z][:], ps[:, XB]).then_inc(x3hi_ready, 1)

            def quad(c, pair, z, last=False):
                Q, n = c * QUADS + 2 * pair + z, c * TILES + 8 * pair + 4 * z
                for j in range(4):
                    act.wait_ge(fc1_full, LEAD + n + j + 1)
                    act.wait_ge(act_ready, LEAD + n + j - 1)
                    nc.scalar.activation(gate[j % 2][:], ps[:, HB + j, 0:HID], ACT.Silu).then_inc(gate_ready, 1)
                    if j == 1 and not last:
                        halve(c, pair + z, 1 - z)
                act.wait_ge(fc2_full, LEAD + n + 4)
                act.wait_ge(y_stored[z], LEAD + 64 * (c * (QUADS // 2) + pair))
                nc.scalar.copy(y[z], ps[:, YB]).then_inc(y_ready, 1)

            def step(o, st):
                kind, i = st[0], st[1]
                if kind == "normT":
                    G, par = 2 * o + i, i % 2
                    act.wait_ge(normT_full, LEAD + G + 1)
                    act.wait_ge(v_full, LEAD + GB * (G - 1))
                    act.wait_ge(qk_full, LEAD + 2 * PAIRS * (G - 1))
                    nc.scalar.copy(xT_hi[par][:], ps[:, ROT]).then_inc(xhi_ready, 1)
                elif kind in ("query", "key"):
                    G, par, pair = 2 * o + i, i % 2, st[2]
                    n = 2 * pair + (kind == "key")
                    act.wait_ge(qk_full, LEAD + 2 * PAIRS * G + n + 1)
                    if n == 0:
                        act.wait_ge(scores_full, LEAD + GB * (G - 1))
                    if kind == "query":
                        nc.scalar.activation(qT[par][:, pair], ps[:, QK], ACT.Identity, bias=bias_q8[:, pair:pair + 1],
                                             scale=HD ** -0.5).then_inc(qk_ready, 1)
                    else:
                        nc.scalar.activation(kT[par][:, pair], ps[:, QK], ACT.Identity, bias=bias_qk[:, 1, pair:pair + 1],
                                             scale=1.0).then_inc(qk_ready, 1)
                elif kind == "value":
                    G, par, j = 2 * o + i, i % 2, st[2]
                    act.wait_ge(v_full, LEAD + GB * G + j + 1)
                    act.wait_ge(mix_full, LEAD + GB * (G - 2) + j + 1)
                    nc.scalar.copy(v[par][:, j], ps[:, ROT]).then_inc(v_ready, 1)
                elif kind == "route_normT":
                    G = 2 * o + i
                    act.wait_ge(x2T_full, LEAD + G + 1)
                    act.wait_ge(logits_full, LEAD + G)
                    nc.scalar.copy(x2T[:], ps[:, ROT]).then_inc(x2T_ready, 1)
                elif kind == "exp":
                    b, par, half = OB * o + i, i % 2, st[2]
                    if half == 0:
                        act.wait_ge(max_ready, LEAD + b + 1)
                        act.wait_ge(pTb_full, LEAD + b - 1)
                        act.wait_ge(mixed_ready, LEAD + b - 1)
                        if i == 1:
                            for z in range(2):
                                act.wait_ge(y_stored[z], LEAD + 64 * (QUADS // 2) * chunk_now[0])
                    for n in range(half * PAIRS, (half + 1) * PAIRS):
                        ins = nc.scalar.activation(probs[par][:, n], masked[par][:, n], ACT.Exp, bias=neg_max[par][:, n:n + 1],
                                                   scale=1.0, accum_out=sums[par][:, n:n + 1])
                    if half == 1:
                        ins.then_inc(probs_ready, 1)
                elif kind == "probsT":
                    b = OB * o + i
                    act.wait_ge(pTa_full, LEAD + b + 1)
                    act.wait_ge(mix_full, LEAD + b)
                    nc.scalar.copy(probsT[:, 0:4], ps[:, PROBST]).then_inc(pTa_ready, 1)
                elif kind == "route_ranks":
                    G = 2 * o + i
                    act.wait_ge(gap_ready, LEAD + G + 1)
                    act.wait_ge(weight1_ready, LEAD + G)
                    nc.scalar.activation(gap_exp[:], gap[:], ACT.Exp).then_inc(gap_exp_ready, 1)
                elif kind == "mixT":
                    b = OB * o + i
                    act.wait_ge(mixT_full, LEAD + b + 1)
                    act.wait_ge(project_full, LEAD + b)
                    nc.scalar.copy(mixedT[:], ps[:, MIXT]).then_inc(mixT_ready, 1)

            for st in first_steps():
                step(0, st)
            act.wait_ge(s_w1, 16 * 5)
            for n in range(2):
                nc.scalar.copy(w1_hi[:, n * EXPERTS * FC1 // 2:(n + 1) * EXPERTS * FC1 // 2],
                               w1_raw[n][:].rearrange("p a b -> p (a b)")).then_inc(s_w1hi, 1)
            act.wait_ge(s_w1lo, 2)

            def chunk(c, before):
                chunk_now[0] = c
                for st in octet_steps(False, before):
                    step(c * per_chunk, st)
                if per_chunk > 1:
                    with act.Fori(1, per_chunk) as i:
                        for st in octet_steps(True, before):
                            step(c * per_chunk + i, st)
                for st in last_steps():
                    step(c * per_chunk + per_chunk - 1, st)
                nc.scalar.activation(table_in[:], zeros[:, 0:1], ACT.Silu).then_inc(silu_in, 1)
                act.wait_ge(silu_in, LEAD + c + 1)
                halve(c, 0, 0)
                each_quad(act, c, quad)

            each_chunk(act, chunk)

        @block.vector
        def _(dve):
            own = [0]

            def link(ins):
                own[0] += 1
                ins.then_inc(s_dve, 1)
                dve.wait_ge(s_dve, own[0])

            V = nc.vector
            dve.wait_ge(s_x, 16)
            xf, up, down, gt = scan
            link(V.tensor_copy(xf[:], x_raw[:]))
            link(V.tensor_scalar(gt[:], xf[:], 39990.0, None, ALU.is_gt))
            link(V.tensor_scalar(up[:], xf[:], 40.0, None, ALU.is_equal))
            link(V.tensor_scalar(down[:], xf[:], 41.0, None, ALU.is_equal))
            for o_, c_ in ((123.0, 125.0), (91.0, 93.0)):
                link(V.scalar_tensor_tensor(up[:], xf[:], o_, up[:], ALU.is_equal, ALU.add))
                link(V.scalar_tensor_tensor(down[:], xf[:], c_, down[:], ALU.is_equal, ALU.add))
            link(V.tensor_tensor(up[:], up[:], down[:], ALU.subtract))
            link(V.memset(xf[:], 0.0))
            link(V.tensor_tensor_scan(down[:], up[:], xf[:], 0.0, ALU.add, ALU.add))
            link(V.tensor_tensor_scan(up[:], gt[:], xf[:], 0.0, ALU.add, ALU.add))
            link(V.tensor_copy(seg_int[:], up[:]))
            link(V.tensor_tensor_scan(gt[:], down[:], down[:], 0.0, ALU.min, ALU.min))
            link(V.tensor_tensor(down[:], down[:], gt[:], ALU.subtract))
            V.tensor_scalar(codes_sb[:, 0], down[:], 0.0, float(NEST - 1), ALU.max, ALU.min).then_inc(s_codes, 1)
            link(V.tensor_scalar(seg_int[:], seg_int[:], SEG - 1, None, ALU.bitwise_and))
            V.tensor_copy(codes_sb[:, 1], seg_int[:]).then_inc(s_codes, 1)
            dve.wait_ge(s_const, 1)
            p = small[:, 0:1]
            acc, cmp_ = small[:, 1:2], small[:, 2:3]
            n3 = PARTS * NEST
            link(V.tensor_copy(part_code[:], p))
            link(V.memset(acc, 0.0))
            for edge, code_step, part_step in ((NEST, -NEST, 1), (2 * NEST, -NEST, 1), (n3, -NEST, -2),
                                               (n3 + SEG, -SEG, 1), (n3 + 2 * SEG, -SEG, 1)):
                link(V.tensor_scalar(cmp_, p, float(edge), None, ALU.is_ge))
                link(V.scalar_tensor_tensor(part_code[:], cmp_, float(code_step), part_code[:], ALU.mult, ALU.add))
                link(V.scalar_tensor_tensor(acc, cmp_, float(part_step), acc, ALU.mult, ALU.add))
            for n in range(PARTS):
                link(V.tensor_scalar(part_mask[:, n:n + 1], acc, float(n), None, ALU.is_equal))
            dve.wait_ge(s_table_ps, 1)
            link(V.tensor_copy(pos_emb[:], ps[:, ROT, 0:D]))
            link(V.tensor_copy(t_full[:], ps[0:CODES, ROT, D:2 * D]))
            link(V.tensor_copy(t_hi[:], t_full[:]))
            link(V.tensor_tensor(t_rest[:], t_full[:], t_hi[:], ALU.subtract))
            link(V.tensor_copy(t_mid[:], t_rest[:]))
            link(V.tensor_tensor(t_rest2[:], t_rest[:], t_mid[:], ALU.subtract))
            link(V.tensor_copy(t_lo[:], t_rest2[:]))
            link(V.tensor_scalar(t_acc[:], t_hi[:], part_mask[:, 0:1], None, ALU.mult))
            link(V.scalar_tensor_tensor(t_acc[:], t_mid[:], part_mask[:, 1:2], t_acc[:], ALU.mult, ALU.add))
            V.scalar_tensor_tensor(code_table[:], t_lo[:], part_mask[:, 2:3], t_acc[:], ALU.mult, ALU.add).then_inc(s_table, 1)
            dve.wait_ge(s_wqkv, 16 * 8)
            V.tensor_copy(bias_v[:], bias_vT[:].unsqueeze(2).broadcast_to([128, PAIRS, S])).then_inc(s_bias_v, 1)
            dve.wait_ge(s_bias_o_ps, 1)
            V.tensor_tensor(bias_o[:], ps[:, ROT, 0:D], bias_o[:], ALU.add).then_inc(s_bias_o, 1)
            dve.wait_ge(s_whi, 2)
            V.tensor_tensor(w_lo[:], w_raw[:], w_hi[:].bitcast(F32), ALU.subtract).then_inc(s_wlo, 1)
            dve.wait_ge(s_bias, 16 * 2 * PARTS)
            nb = PARTS * EXPERTS
            link(V.tensor_scalar(small[0:nb, 1:2], small[0:nb, 0:1], float(EXPERTS), None, ALU.is_ge))
            link(V.tensor_scalar(small[0:nb, 2:3], small[0:nb, 0:1], float(2 * EXPERTS), None, ALU.is_ge))
            link(V.tensor_tensor(small[0:nb, 3:4], small[0:nb, 1:2], small[0:nb, 2:3], ALU.add))
            for n in range(PARTS):
                link(V.tensor_scalar(b_mask[:, n:n + 1], small[0:nb, 3:4], float(n), None, ALU.is_equal))
            link(V.tensor_copy(b_hi[:], b12[:]))
            link(V.tensor_tensor(b_rest[:], b12[:], b_hi[:], ALU.subtract))
            link(V.tensor_copy(b_mid[:], b_rest[:]))
            link(V.tensor_tensor(b_rest[:], b_rest[:], b_mid[:], ALU.subtract))
            link(V.tensor_scalar(b_rest[:], b_rest[:], b_mask[:, 2:3], None, ALU.mult))
            link(V.scalar_tensor_tensor(b_rest[:], b_mid[:], b_mask[:, 1:2], b_rest[:], ALU.mult, ALU.add))
            V.scalar_tensor_tensor(b_parts[:], b_hi[:], b_mask[:, 0:1], b_rest[:], ALU.mult, ALU.add).then_inc(s_bparts, 1)
            dve.wait_ge(s_table, 1)
            dve.wait_ge(s_pool, 1)

            def step(o, st):
                kind, i = st[0], st[1]
                G, b, par = 2 * o + i, OB * o + i, i % 2
                if kind == "onehot":
                    dve.wait_ge(codes_in[par], LEAD + 16 * (G - par + 2))
                    dve.wait_ge(embed_full, LEAD + G)
                    V.tensor_scalar(onehot[:], code_rows[par][:], part_code[:], None, ALU.is_equal).then_inc(onehot_ready, 1)
                elif kind == "embed":
                    dve.wait_ge(embed_full, LEAD + G + 1)
                    dve.wait_ge(residual_ready, LEAD + G - 1)
                    V.tensor_tensor(h[par][:], ps[:, ROT].rearrange("p (j d) -> p j d", j=GB),
                                    pos_emb[:].unsqueeze(1).broadcast_to([S, GB, D]), ALU.add).then_inc(embedded, 1)
                    dve.wait_ge(embedded, LEAD + G + 1)
                    dve.wait_ge(normed_ready, LEAD + G)
                    for j in range(GB):
                        ins = V.bn_stats(stats[:, j], h[par][:, j])
                    ins.then_inc(bn_done, 1)
                    dve.wait_ge(bn_done, LEAD + G + 1)
                    carry_wait(dve)
                    for j in range(GB):
                        ins = V.bn_aggr(moments[:, j], stats[:, j])
                    ins.then_inc(moments_ready, 1)
                elif kind == "norm":
                    dve.wait_ge(rstd_ready, LEAD + G + 1)
                    dve.wait_ge(normT_full, LEAD + G)
                    for j in range(GB):
                        ins = V.tensor_scalar(normed[:, j], h[par][:, j], moments[:, j, 0:1], rstd[:, j:j + 1],
                                              ALU.subtract, ALU.mult)
                    ins.then_inc(normed_ready, 1)
                elif kind == "normT":
                    dve.wait_ge(xhi_ready, LEAD + G + 1)
                    V.tensor_tensor(xT_lo[par][:], ps[:, ROT], xT_hi[par][:].bitcast(F32), ALU.subtract).then_inc(xlo_ready, 1)
                elif kind == "scores":
                    dve.wait_ge(scores_full, LEAD + b + 1)
                    dve.wait_ge(probs_ready, LEAD + b - 1)
                    V.tensor_tensor(masked[par][:], ps[:, SCORES:SCORES + 2].rearrange("p a (n k) -> p (a n) k", n=4),
                                    causal[:].unsqueeze(1).broadcast_to([S, HEADS, S]), ALU.min).then_inc(masked_ready, 1)
                elif kind == "max":
                    dve.wait_ge(masked_ready, LEAD + b + 1)
                    V.tensor_reduce(neg_max[par][:], masked[par][:], AX, ALU.max, negate=True).then_inc(max_ready, 1)
                elif kind == "probsT":
                    dve.wait_ge(pTb_full, LEAD + b + 1)
                    dve.wait_ge(mix_full, LEAD + b)
                    V.tensor_copy(probsT[:, 4:8], ps[:, PROBST + 1].rearrange("p (n k) -> p n k", n=4)).then_inc(pTb_ready, 1)
                    dve.wait_ge(probs_ready, LEAD + b + 1)
                    V.reciprocal(inv_sums[:], sums[par][:]).then_inc(inv_ready, 1)
                elif kind == "mix":
                    dve.wait_ge(inv_ready, LEAD + b + 1)
                    dve.wait_ge(mix_full, LEAD + b + 1)
                    dve.wait_ge(mixT_full, LEAD + b)
                    V.tensor_tensor(mixed[:].rearrange("p (m e d) -> p e m d", e=2, d=HD),
                                    ps[:, MIX].rearrange("p (m e d) -> p e m d", e=2, d=HD),
                                    inv_sums[:].rearrange("p (e m) -> p e m", e=2).unsqueeze(3).broadcast_to([S, 2, PAIRS, HD]),
                                    ALU.mult).then_inc(mixed_ready, 1)
                elif kind == "project":
                    j, hp = i % GB, (i // GB) % 2
                    dve.wait_ge(project_full, LEAD + b + 1)
                    if j == 0:
                        dve.wait_ge(h2_stored[hp], LEAD + 16 * group_turn(o, i))
                    if j == 0:
                        dve.wait_ge(residual_ready, LEAD + 2 * o + (i // GB) + 1)
                        dve.wait_ge(normed2_ready, LEAD + 2 * o + (i // GB) - 1)
                    V.tensor_tensor(h2[hp][:, j], ps[:, ROT, 0:D], residual[hp][:, j], ALU.add).then_inc(h2_ready, 1)
                elif kind == "route_norm":
                    dve.wait_ge(h2_ready, LEAD + GB * (G + 1))
                    dve.wait_ge(moments2_ready, LEAD + G)
                    for j in range(GB):
                        ins = V.bn_stats(stats2[:, j], h2[par][:, j])
                    ins.then_inc(bn2_done, 1)
                    dve.wait_ge(bn2_done, LEAD + G + 1)
                    dve.wait_ge(normed2_ready, LEAD + G)
                    carry_wait(dve)
                    for j in range(GB):
                        ins = V.bn_aggr(moments2[:, j], stats2[:, j])
                    ins.then_inc(moments2_ready, 1)
                elif kind == "route_scale":
                    dve.wait_ge(rstd2_ready, LEAD + G + 1)
                    dve.wait_ge(scattered[par], SW_LEAD + 16 * 2 * GB * (o + (i - par) // 2))
                    dve.wait_ge(x2T_full, LEAD + G - 1)
                    for j in range(GB):
                        ins = V.tensor_scalar(normed2[par][:, j], h2[par][:, j], moments2[:, j, 0:1], rstd2[:, j:j + 1],
                                              ALU.subtract, ALU.mult)
                    ins.then_inc(normed2_ready, 1)
                elif kind == "route_logits":
                    dve.wait_ge(logits_full, LEAD + G + 1)
                    dve.wait_ge(top_at_ready, LEAD + G)
                    V.tensor_tensor(logits[:], ps[:, ROT, 0:GB * EXPERTS].rearrange("p (j e) -> p j e", j=GB),
                                    bias_r[:].unsqueeze(1).broadcast_to([S, GB, EXPERTS]), ALU.add).then_inc(logits_ready, 1)
                    dve.wait_ge(logits_ready, LEAD + G + 1)
                    dve.wait_ge(gap_ready, LEAD + G)
                    carry_wait(dve)
                    for j in range(GB):
                        ins = V.max(top[:, j], logits[:, j])
                    ins.then_inc(top_ready, 1)
                    dve.wait_ge(top_ready, LEAD + G + 1)
                    dve.wait_ge(top_no_ready, LEAD + G)
                    carry_wait(dve)
                    for j in range(GB):
                        ins = V.max_index(top_at[:, j], top[:, j], logits[:, j])
                    ins.then_inc(top_at_ready, 1)
                elif kind == "route_choose":
                    dve.wait_ge(gap_exp_ready, LEAD + G)
                    V.tensor_tensor(gap[:], top[:, :, 1], top[:, :, 0], ALU.subtract).then_inc(gap_ready, 1)
                    dve.wait_ge(top_at_ready, LEAD + G + 1)
                    dve.wait_ge(chosen_ready, LEAD + 2 * G)
                    V.tensor_copy(top_no[:], top_at[:, :, 0:2]).then_inc(top_no_ready, 1)
                    dve.wait_ge(top_no_ready, LEAD + G + 1)
                    dve.wait_ge(picked_ready, LEAD + G)
                    dve.wait_ge(rows_a, LEAD + 2 * G)
                    for k in range(2):
                        V.tensor_tensor(chosen[:, k], expert_no[:].unsqueeze(1).broadcast_to([S, GB, EXPERTS]),
                                        top_no[:, :, k:k + 1].broadcast_to([S, GB, EXPERTS]), ALU.is_equal).then_inc(chosen_ready, 1)
                elif kind == "route_weight":
                    dve.wait_ge(gap_exp_ready, LEAD + G + 1)
                    V.tensor_scalar(gap_one[:], gap_exp[:], 1.0, None, ALU.add).then_inc(gap_one_ready, 1)
                    dve.wait_ge(gap_one_ready, LEAD + G + 1)
                    dve.wait_ge(weights_kept, LEAD + G)
                    V.reciprocal(weight[:, 0], gap_one[:]).then_inc(weight0_ready, 1)
                    dve.wait_ge(weight0_ready, LEAD + G + 1)
                    V.tensor_tensor(weight[:, 1], gap_exp[:], weight[:, 0], ALU.mult).then_inc(weight1_ready, 1)
                elif kind == "route_ranks":
                    dve.wait_ge(ranks_full, LEAD + G + 1)
                    dve.wait_ge(rows_c, LEAD + G)
                    V.tensor_copy(ranks[:], ps[:, ROT, 0:2 * GB * EXPERTS].rearrange("p (a j e) -> p a j e", a=2, j=GB)).then_inc(ranks_ready, 1)
                elif kind == "route_rows":
                    dve.wait_ge(rows_a, LEAD + 2 * (G + 1))
                    dve.wait_ge(row_ready, LEAD + G)
                    V.tensor_reduce(row_f[:], rows_2[:], AX, ALU.add).then_inc(rows_b, 1)
                    dve.wait_ge(rows_b, LEAD + G + 1)
                    dve.wait_ge(scattered[par], SW_LEAD + 16 * 2 * GB * (o + (i - par) // 2))
                    dve.wait_ge(rows_kept, LEAD + G - 1)
                    V.tensor_copy(row[par][:], row_f[:]).then_inc(row_ready, 1)

            def group_turn(o, i):
                return o + (0 if i >= 0 else -1)

            def table(c):
                dve.wait_ge(ends_ready, LEAD + c + 1)
                n = [0]

                def link(ins):
                    n[0] += 1
                    ins.then_inc(table_own, 1)
                    dve.wait_ge(table_own, LEAD + c * TABLE_STEPS + n[0])

                link(V.tensor_copy(tiles_f[:], ends[:]))
                link(V.tensor_tensor(tiles_f[:], tiles_f[:], region[0:1], ALU.subtract))
                link(V.tensor_scalar(tiles_i[:], tiles_f[:], float(S - 1), None, ALU.add))
                link(V.tensor_scalar(tiles_i[:], tiles_i[:], 7, None, ALU.logical_shift_right))
                link(V.tensor_copy(tiles_f[:], tiles_i[:]))
                link(V.tensor_tensor_scan(tiles_end[:], tiles_f[:], tab[:, 3, 0:EXPERTS], 0.0, ALU.add, ALU.add))
                link(V.tensor_tensor(passed[:], tile_no[:].unsqueeze(2).broadcast_to([1, TILES, EXPERTS]),
                                     tiles_end[:].unsqueeze(1).broadcast_to([1, TILES, EXPERTS]), ALU.is_ge))
                link(V.tensor_reduce(tab[:, 0], passed[:], AX, ALU.add))
                link(V.tensor_tensor(passed[:], passed[:], tiles_f[:].unsqueeze(1).broadcast_to([1, TILES, EXPERTS]), ALU.mult))
                link(V.tensor_reduce(tab[:, 1], passed[:], AX, ALU.add))
                link(V.tensor_tensor(tab[:, 1], tile_no[:], tab[:, 1], ALU.subtract))
                link(V.scalar_tensor_tensor(tab[:, 1], tab[:, 0], float(R // S), tab[:, 1], ALU.mult, ALU.add))
                by_two = tab[:, 1].rearrange("p (q j) -> p q j", j=2)
                link(V.scalar_tensor_tensor(blocks_f[:], by_two[:, :, 1], 512.0, by_two[:, :, 0], ALU.mult, ALU.add))
                link(V.tensor_scalar(experts_f[:], tab[:, 0], float(EXPERTS - 1), None, ALU.min))
                by_quad = experts_f[:].rearrange("p (q j) -> p q j", j=4)
                link(V.scalar_tensor_tensor(packed[:], by_quad[:, :, 3], 16.0, by_quad[:, :, 2], ALU.mult, ALU.add))
                link(V.scalar_tensor_tensor(packed[:], packed[:], 16.0, by_quad[:, :, 1], ALU.mult, ALU.add))
                link(V.scalar_tensor_tensor(packed[:], packed[:], 16.0, by_quad[:, :, 0], ALU.mult, ALU.add))
                assert n[0] == TABLE_STEPS
                V.tensor_copy(tile_blocks[:], blocks_f[:]).then_inc(table_ready, 1)
                V.tensor_copy(quad_experts[:], packed[:]).then_inc(table_ready, 1)

            def rest(c, pair, z):
                Q = c * QUADS + 2 * pair + z
                dve.wait_ge(x3hi_ready, LEAD + Q + 1)
                V.tensor_tensor(x3_lo[z][:], ps[:, XB], x3_hi[z][:].bitcast(F32), ALU.subtract).then_inc(x3lo_ready, 1)

            def quad(c, pair, z, last=False):
                n = c * TILES + 8 * pair + 4 * z

                def act(j):
                    dve.wait_ge(gate_ready, LEAD + n + j + 1)
                    V.tensor_tensor(act_out[j], gate[j % 2][:], ps[:, HB + j, HID:FC1], ALU.mult).then_inc(act_ready, 1)

                def actT_out(j):
                    dve.wait_ge(actT_full, LEAD + n + j + 1)
                    if j == 0:
                        dve.wait_ge(fc2_full, LEAD + n)
                    V.tensor_copy(actT[j], ps[:, AB + j % 2, 0:HID].rearrange("p (a s) -> p a s", a=2)).then_inc(actT_ready, 1)

                act(0)
                act(1)
                actT_out(0)
                if not last:
                    rest(c, pair + z, 1 - z)
                act(2)
                actT_out(1)
                act(3)
                actT_out(2)
                actT_out(3)

            def add(o, j):
                half = j // GB
                dve.wait_ge(y_in[j % 4], SW_LEAD + 32 * (2 * o + half + 1))
                if j % GB == 0:
                    dve.wait_ge(h_in[half], LEAD + 16 * (o + 1))
                if j == 0:
                    dve.wait_ge(weights_now_ready, LEAD + o + 1)
                rows = total[half][:, j % GB]
                V.scalar_tensor_tensor(rows, y_rows[j % 4][:, 0], weights_now[:, 0, j:j + 1], rows, ALU.mult, ALU.add).then_inc(half_total, 1)
                dve.wait_ge(half_total, LEAD + OB * o + j + 1)
                V.scalar_tensor_tensor(rows, y_rows[j % 4][:, 1], weights_now[:, 1, j:j + 1], rows, ALU.mult, ALU.add).then_inc(total_ready, 1)

            link(V.memset(tab[:, 3], 0.0))
            for st in first_steps():
                step(0, st)
            for n in range(2):
                dve.wait_ge(s_w1hi, n + 1)
                cols = slice(n * EXPERTS * FC1 // 2, (n + 1) * EXPERTS * FC1 // 2)
                V.tensor_tensor(w1_lo[:, cols], w1_raw[n][:].rearrange("p a b -> p (a b)"), w1_hi[:, cols].bitcast(F32),
                                ALU.subtract).then_inc(s_w1lo, 1)

            def octet(c, i, steps):
                for st in steps:
                    step(c * per_chunk + i, st)
                    if st[0] == "total":
                        add((c - 1) * per_chunk + i, st[1])

            def chunk(c, before):
                octet(c, 0, octet_steps(False, before))
                if per_chunk > 1:
                    with dve.Fori(1, per_chunk) as i:
                        octet(c, i, octet_steps(True, before))
                octet(c, per_chunk - 1, last_steps())
                table(c)
                rest(c, 0, 0)
                each_quad(dve, c, quad)

            each_chunk(dve, chunk)
            with dve.Fori(0, per_chunk) as i:
                for j in range(OB):
                    add((chunks - 1) * per_chunk + i, j)

        @block.tensor
        def _(pe):
            T = nc.tensor
            pe.wait_ge(s_w, 16 * 4)
            T.matmul(ps[:, ROT, 0:D], posT[:], w_emb[:, 0], start=True, stop=True, skip_group_check=True)
            T.matmul(ps[0:CODES, ROT, D:2 * D], nestT[:], w_emb[:, 1], start=False, stop=False, skip_group_check=True)
            T.matmul(ps[0:CODES, ROT, D:2 * D], segT[:], w_emb[:, 2], start=False, stop=True, skip_group_check=True).then_inc(s_table_ps, 1)
            pe.wait_ge(s_table, 1)
            pe.wait_ge(s_bias_v, 1)
            for n in range(PAIRS):
                ins = T.matmul(ps[:, ROT, 0:D], bias_v[:, n], w_o[:, n], start=(n == 0), stop=(n == PAIRS - 1))
            ins.then_inc(s_bias_o_ps, 1)
            pe.wait_ge(s_bias_o, 1)
            pe.wait_ge(s_wlo, 1)
            pe.wait_ge(s_pool, 1)

            def three(dst, w_hi_, w_lo_, x_hi_, x_lo_):
                T.matmul(dst, w_hi_, x_hi_, start=True, stop=False)
                T.matmul(dst, w_hi_, x_lo_, start=False, stop=False)
                return T.matmul(dst, w_lo_, x_hi_, start=False, stop=True)

            rot_free = {}

            def step(o, st, last_rot):
                kind, i = st[0], st[1]
                G, b, par = 2 * o + i, OB * o + i, i % 2

                def wait_rot():
                    k, n = last_rot[0], last_rot[1]
                    if k == "embed":
                        pe.wait_ge(embedded, LEAD + 2 * o + n + 1)
                    elif k == "normT":
                        pe.wait_ge(xlo_ready, LEAD + 2 * o + n + 1)
                    elif k == "value":
                        pe.wait_ge(v_ready, LEAD + GB * (2 * o + n) + last_rot[2] + 1)
                    elif k == "project":
                        pe.wait_ge(h2_ready, LEAD + OB * o + n + 1)
                    elif k == "route_normT":
                        pe.wait_ge(x2T_ready, LEAD + 2 * o + n + 1)
                    elif k == "route_logits":
                        pe.wait_ge(logits_ready, LEAD + 2 * o + n + 1)
                    elif k == "route_ranks":
                        pe.wait_ge(ranks_ready, LEAD + 2 * o + n + 1)

                if kind == "embed":
                    wait_rot()
                    pe.wait_ge(onehot_ready, LEAD + G + 1)
                    for j in range(GB):
                        ins = T.matmul(ps[:, ROT, j * D:(j + 1) * D], onehot[:, j * S:(j + 1) * S], code_table[:],
                                       start=True, stop=True)
                    ins.then_inc(embed_full, 1)
                elif kind == "normT":
                    wait_rot()
                    pe.wait_ge(normed_ready, LEAD + G + 1)
                    for j in range(GB):
                        ins = T.transpose(ps[:, ROT, j * S:(j + 1) * S], normed[:, j], ident[:])
                    ins.then_inc(normT_full, 1)
                elif kind in ("query", "key"):
                    pair = st[2]
                    n = 2 * pair + (kind == "key")
                    w = int(kind == "key")
                    if n == 0:
                        pe.wait_ge(xlo_ready, LEAD + G + 1)
                    pe.wait_ge(qk_ready, LEAD + 2 * PAIRS * G + n)
                    cols = slice(pair * 128, (pair + 1) * 128)
                    three(ps[:, QK], w_hi[:, w, cols], w_lo[:, w, cols], xT_hi[par][:], xT_lo[par][:]).then_inc(qk_full, 1)
                elif kind == "value":
                    j = st[2]
                    wait_rot()
                    if j == 0:
                        pe.wait_ge(xlo_ready, LEAD + G + 1)
                    cols = slice(j * S, (j + 1) * S)
                    three(ps[:, ROT], xT_hi[par][:, cols], xT_lo[par][:, cols], w_hi[:, 2], w_lo[:, 2]).then_inc(v_full, 1)
                elif kind == "scores":
                    j, gp = i % GB, (i // GB) % 2
                    if j == 0:
                        pe.wait_ge(qk_ready, LEAD + 2 * PAIRS * (2 * o + i // GB + 1))
                    pe.wait_ge(masked_ready, LEAD + b)
                    cols = slice(j * S, (j + 1) * S)
                    for pair in range(PAIRS):
                        for e in range(2):
                            rows = slice(e * HD, (e + 1) * HD)
                            ins = T.matmul(ps[:, SCORES + e, pair * S:(pair + 1) * S], qT[gp][rows, pair, cols],
                                           kT[gp][rows, pair, cols], start=True, stop=True)
                    ins.then_inc(scores_full, 1)
                elif kind == "probsT":
                    pe.wait_ge(probs_ready, LEAD + b + 1)
                    pe.wait_ge(pTa_ready, LEAD + b)
                    pe.wait_ge(pTb_ready, LEAD + b)
                    for n in range(HEADS):
                        ins = T.transpose(ps[:, PROBST + n // 4, (n % 4) * S:(n % 4 + 1) * S], probs[par][:, n], ident[:])
                        if n == 3:
                            ins.then_inc(pTa_full, 1)
                    ins.then_inc(pTb_full, 1)
                elif kind == "mix":
                    j, gp = i % GB, (i // GB) % 2
                    if j == 0:
                        pe.wait_ge(v_ready, LEAD + GB * (2 * o + i // GB + 1))
                    pe.wait_ge(pTa_ready, LEAD + b + 1)
                    pe.wait_ge(pTb_ready, LEAD + b + 1)
                    pe.wait_ge(mixed_ready, LEAD + b)
                    for n in range(HEADS):
                        head = 2 * (n % PAIRS) + n // PAIRS
                        ins = T.matmul(ps[:, MIX, head * HD:(head + 1) * HD], probsT[:, n], v[gp][:, j, head * HD:(head + 1) * HD],
                                       start=True, stop=True)
                    ins.then_inc(mix_full, 1)
                elif kind == "mixT":
                    pe.wait_ge(mixed_ready, LEAD + b + 1)
                    pe.wait_ge(mixT_ready, LEAD + b)
                    for n in range(PAIRS):
                        ins = T.transpose(ps[:, MIXT, n * S:(n + 1) * S], mixed[:, n * 128:(n + 1) * 128], ident[:])
                    ins.then_inc(mixT_full, 1)
                elif kind == "project":
                    wait_rot()
                    pe.wait_ge(mixT_ready, LEAD + b + 1)
                    for n in range(PAIRS):
                        ins = T.matmul(ps[:, ROT, 0:D], mixedT[:, n], w_o[:, n], start=(n == 0), stop=(n == PAIRS - 1))
                    ins.then_inc(project_full, 1)
                elif kind == "route_normT":
                    wait_rot()
                    pe.wait_ge(normed2_ready, LEAD + G + 1)
                    for j in range(GB):
                        ins = T.transpose(ps[:, ROT, j * S:(j + 1) * S], normed2[par][:, j], ident[:])
                    ins.then_inc(x2T_full, 1)
                elif kind == "route_logits":
                    wait_rot()
                    pe.wait_ge(s_w1, 16 * 5)
                    pe.wait_ge(x2T_ready, LEAD + G + 1)
                    for j in range(GB):
                        ins = T.matmul(ps[:, ROT, j * EXPERTS:(j + 1) * EXPERTS], x2T[:, j * S:(j + 1) * S], w_router[:],
                                       start=True, stop=True)
                    ins.then_inc(logits_full, 1)
                elif kind == "route_ranks":
                    wait_rot()
                    pe.wait_ge(picked_ready, LEAD + G + 1)
                    n = GB * EXPERTS
                    T.matmul(ps[:, ROT, 0:n], earlier[:], picked[:].rearrange("p j e -> p (j e)"), start=True, stop=True)
                    T.matmul(ps[:, ROT, n:2 * n], ones[:], picked[:].rearrange("p j e -> p (j e)"), start=True,
                             stop=True).then_inc(ranks_full, 1)

            expert = {}

            def rows_in(c, pair, z):
                Q = c * QUADS + 2 * pair + z
                pe.wait_ge(xt_in[z], LEAD + 64 * (c * (QUADS // 2) + pair + 1))
                for j in range(4):
                    ins = T.transpose(ps[:, XB, j * S:(j + 1) * S], xt[z][:, j], ident[:])
                ins.then_inc(x3T_full, 1)

            def tiles(c, pair, z):
                Q, n = c * QUADS + 2 * pair + z, c * TILES + 8 * pair + 4 * z
                def load_experts():
                    e = pe.value_load(quad_experts[0:1, bass.ds(2 * pair + z, 1)], min_val=0, max_val=0x7777)
                    for j in range(4):
                        expert[z, j] = (e >> (4 * j)) & (EXPERTS - 1)

                def fc1(j):
                    e = expert[z, j]
                    cols, rows = bass.ds(e * FC1, FC1), slice(j * S, (j + 1) * S)
                    if j == 0:
                        pe.wait_ge(x3lo_ready, LEAD + Q + 1)
                    T.matmul(ps[:, HB + j], ones[0:PARTS], b1_parts[:, cols], start=True, stop=False)
                    T.matmul(ps[:, HB + j], x3_hi[z][:, rows], w1_hi[:, cols], start=False, stop=False)
                    T.matmul(ps[:, HB + j], x3_lo[z][:, rows], w1_hi[:, cols], start=False, stop=False)
                    T.matmul(ps[:, HB + j], x3_hi[z][:, rows], w1_lo[:, cols], start=False, stop=True).then_inc(fc1_full, 1)

                def transpose(j):
                    pe.wait_ge(act_ready, LEAD + n + j + 1)
                    for half in range(2):
                        ins = T.transpose(ps[:, AB + j % 2, half * S:(half + 1) * S], act_out[j][:, half * 128:(half + 1) * 128], ident[:])
                    ins.then_inc(actT_full, 1)

                def fc2(j):
                    e = expert[z, j]
                    dst = ps[:, YB, j * D:(j + 1) * D]
                    if j == 0:
                        pe.wait_ge(y_ready, LEAD + Q)
                    pe.wait_ge(actT_ready, LEAD + n + j + 1)
                    T.matmul(dst, ones[0:PARTS], b2_parts[:, bass.ds(e * D, D)], start=True, stop=False)
                    for half in range(2):
                        ins = T.matmul(dst, actT[j][:, half], w2[:, bass.ds(e * 2 * D + half * D, D)],
                                       start=False, stop=(half == 1))
                    ins.then_inc(fc2_full, 1)

                return load_experts, fc1, transpose, fc2


            def start_quad(c, pair, z, last=False):
                load_experts, fc1, transpose, fc2 = tiles(c, pair, z)
                fc1(0)
                fc1(1)
                if not last:
                    rows_in(c, pair + z, 1 - z)

            def finish_quad(c, pair, z, last=False):
                load_experts, fc1, transpose, fc2 = tiles(c, pair, z)
                if z == 0:
                    load_experts()
                transpose(0)
                fc1(2)
                transpose(1)
                fc2(0)
                fc1(3)
                if not last:
                    tiles(c, pair + z, 1 - z)[0]()
                transpose(2)
                fc2(1)
                transpose(3)
                fc2(2)
                fc2(3)

            ROT_STEPS = ("embed", "normT", "value", "project", "route_normT", "route_logits", "route_ranks")

            last_rot = [st for st in octet_steps(True, False) if st[0] in ROT_STEPS][-1]

            def next_octet(st):
                return (st[0], st[1] - (OB if st[0] == "project" else 2), *st[2:])

            def run(o, steps, before):
                for st in steps:
                    step(o, st, before)
                    if st[0] in ROT_STEPS:
                        before = st

            run(0, first_steps(),
                ("value", -1, 3))

            def chunk(c, before):
                run(c * per_chunk, octet_steps(False, before), ("value", 0, 3))
                if per_chunk > 1:
                    with pe.Fori(1, per_chunk) as i:
                        run(c * per_chunk + i, octet_steps(True, before), next_octet(last_rot))
                run(c * per_chunk + per_chunk - 1, last_steps(), last_rot)
                pe.wait_ge(ranks_ready, LEAD + 2 * per_chunk * (c + 1))
                pe.wait_ge(table_ready, LEAD + 2 * (c + 1))
                pe.wait_ge(s_w1, 16 * 5)
                pe.wait_ge(s_bmoved, 16 * 2 * PARTS)
                rows_in(c, 0, 0)
                tiles(c, 0, 0)[0]()
                start_quad(c, 0, 0)
                with pe.Fori(0, QUADS // 2 - 1) as pair:
                    finish_quad(c, pair, 0)
                    start_quad(c, pair, 1)
                    finish_quad(c, pair, 1)
                    start_quad(c, pair + 1, 0)
                finish_quad(c, QUADS // 2 - 1, 0)
                start_quad(c, QUADS // 2 - 1, 1, last=True)
                finish_quad(c, QUADS // 2 - 1, 1, last=True)
                pe.wait_ge(y_ready, LEAD + QUADS * (c + 1))

            each_chunk(pe, chunk)


def kernel(**i):
    import concourse.bacc as bacc
    from concourse.bass_utils import run_bass_kernel_spmd as run
    nc = bacc.Bacc("TRN2", target_bir_lowering=False, num_devices=1)
    i = {k: np.asarray(v) for k, v in i.items()}
    nseq = i["x"].shape[0]
    nest, seg = i["L0_tok_nest_table"].T, i["L0_tok_seg_table"].T
    laid = {
        "x": i["x"],
        "posT": i["L0_tok_pos_table"][:S].T,
        "w_emb": i["L0_tok_W"],
        "nestT": np.concatenate([nest] * PARTS + [np.zeros((128, PARTS * SEG), nest.dtype)], axis=1),
        "segT": np.concatenate([np.zeros((128, PARTS * NEST), seg.dtype)] + [seg] * PARTS, axis=1),
        "wq": i["L0_attn_wq"].reshape(D, -1), "wk": i["L0_attn_wk"].reshape(D, -1), "wv": i["L0_attn_wv"].reshape(D, -1),
        "bq": i["L0_attn_bq"].reshape(PAIRS, 128).T, "bk": i["L0_attn_bk"].reshape(PAIRS, 128).T,
        "bv": i["L0_attn_bv"].reshape(PAIRS, 128).T, "bo": i["L0_attn_bo"].reshape(1, -1),
        "wo": i["L0_attn_wo"].reshape(-1, D),
        "wr": i["L0_ffn_router_w"].T, "br": i["L0_ffn_router_b"].reshape(1, -1),
        "w1": i["L0_ffn_fc1_w"].transpose(2, 0, 1).reshape(D, -1),
        "w2": i["L0_ffn_fc2_w"].reshape(EXPERTS, D, 2, 128).transpose(3, 0, 2, 1).reshape(128, -1),
        "b1": i["L0_ffn_fc1_b"], "b2": i["L0_ffn_fc2_b"],
    }
    laid = {k: np.ascontiguousarray(v) for k, v in laid.items()}
    a = {k: nc.dram_tensor("in_" + k, v.shape, mybir.dt.from_np(v.dtype), kind="ExternalInput").ap() for k, v in laid.items()}
    out = nc.dram_tensor("out_h", (nseq, S, D), mybir.dt.float32, kind="ExternalOutput").ap()
    hmid = nc.dram_tensor("hmid", (nseq, S, D), mybir.dt.float32, kind="Internal").ap()
    rows = EXPERTS * ((nseq // (4 if nseq == 128 else 2)) * S + S) + EXPERTS * S
    xs = nc.dram_tensor("xs", (rows, D), mybir.dt.float32, kind="Internal").ap()
    spare = nc.dram_tensor("spare", (6, D), mybir.dt.float32, kind="Internal").ap()
    ys = nc.dram_tensor("ys", (rows, D), mybir.dt.float32, kind="Internal").ap()
    codes = nc.dram_tensor("codes", (2, (nseq + OB) * S), mybir.dt.bfloat16, kind="Internal").ap()
    build(nc, a, out, hmid, codes, xs, ys, spare, nseq)
    r = run(nc, [{"in_" + k: v for k, v in laid.items()}], core_ids=[0])
    return r.results[0]["out_h"]
```
